# Optimizing a Trainium2 kernel written in Bass

```python
import numpy as np
import jax
import jax.numpy as jnp

def _softmax(x, axis=-1):
    return jax.nn.softmax(x, axis=axis)
def _gelu(x):
    return jax.nn.gelu(x, approximate=True)
def _silu(x):
    return jax.nn.silu(x)
def _sigmoid(x):
    return jax.nn.sigmoid(x)
def _layernorm(x, axis=-1, eps=1e-5):
    m = jnp.mean(x, axis=axis, keepdims=True)
    v = jnp.var(x, axis=axis, keepdims=True)
    return (x - m) / jnp.sqrt(v + eps)
def _scatter_add(tgt, idx, src, axis=0):
    return tgt.at[idx].add(src)
def _segment_sum(src, seg, n):
    return jax.ops.segment_sum(src, seg, n)

kernel_name = 'mk_adj_seq_d1_adj_256_0780d2'

def setup_inputs(seed: int = 0):
    np.random.seed(seed)
    _w = jnp.asarray
    def _rec_inputs():
        import jax
        import jax.numpy as jnp
        _gk = jax.random.key(seed)
        x = -9.806e-05 + 1 * jax.random.normal(jax.random.fold_in(_gk, 1), (16, 1024, 256), jnp.float32)
        _a = jax.random.bernoulli(jax.random.fold_in(_gk, 2), 0.03125, (1024, 1024))
        _a = jnp.logical_or(_a, jnp.swapaxes(_a, -1, -2))
        _a = jnp.logical_or(_a, jnp.eye(1024, dtype=bool))
        _af = _a.astype(jnp.float32)
        _af = _af * jax.random.uniform(jax.random.fold_in(_gk, 3), (1024, 1024), jnp.float32, 0.05, 0.189921)
        adj = _af
        return x, adj
    x, adj = _rec_inputs()
    def _L0_gnn_setup():
        import jax, jax.numpy as jnp
        import numpy as np
        B, C, D = (16, 128, 256)
        key = jax.random.key(seed)
        ks = jax.random.split(key, 12)
        s = 0.05
        return {'h_t': jax.random.normal(ks[0], (B, C, D), jnp.float32), 'A_a': jax.random.normal(ks[1], (C, C), jnp.float32) * s, 'A_m': jax.random.normal(ks[2], (C, C), jnp.float32) * s, 'W1': jax.random.normal(ks[3], (2 * D, D), jnp.float32) * s, 'b1': jax.random.normal(ks[4], (D,), jnp.float32) * s, 'W2': jax.random.normal(ks[5], (D, 1), jnp.float32) * s, 'b2': jax.random.normal(ks[6], (1,), jnp.float32) * s, 'Wa': jax.random.normal(ks[7], (D, D), jnp.float32) * s, 'ba': jax.random.normal(ks[8], (D,), jnp.float32) * s, 'Wm': jax.random.normal(ks[9], (D, D), jnp.float32) * s, 'bm': jax.random.normal(ks[10], (D,), jnp.float32) * s, 'beta1': jnp.float32(1.0), 'beta2': jnp.float32(1.0), 'beta3': jnp.float32(1.0)}
    _L0_gnn_all = _L0_gnn_setup()
    _L0_gnn_in = {k: v for k, v in _L0_gnn_all.items() if k in ('W1', 'b1', 'W2', 'b2', 'Wa', 'ba', 'Wm', 'bm', 'beta1', 'beta2', 'beta3', )}
    del _L0_gnn_all

    return {
        "x": x,
        "adj": adj,
        "L0_gnn_W1": _L0_gnn_in["W1"],
        "L0_gnn_b1": _L0_gnn_in["b1"],
        "L0_gnn_W2": _L0_gnn_in["W2"],
        "L0_gnn_b2": _L0_gnn_in["b2"],
        "L0_gnn_Wa": _L0_gnn_in["Wa"],
        "L0_gnn_ba": _L0_gnn_in["ba"],
        "L0_gnn_Wm": _L0_gnn_in["Wm"],
        "L0_gnn_bm": _L0_gnn_in["bm"],
        "L0_gnn_beta1": _L0_gnn_in["beta1"],
        "L0_gnn_beta2": _L0_gnn_in["beta2"],
        "L0_gnn_beta3": _L0_gnn_in["beta3"],
    }

def reference(x, adj, L0_gnn_W1, L0_gnn_b1, L0_gnn_W2, L0_gnn_b2, L0_gnn_Wa, L0_gnn_ba, L0_gnn_Wm, L0_gnn_bm, L0_gnn_beta1, L0_gnn_beta2, L0_gnn_beta3):
    import jax
    import jax.numpy as jnp
    def _L0_gnn_ref(h_t, A_a, A_m, W1, b1, W2, b2, Wa, ba, Wm, bm, beta1, beta2, beta3):
        import jax, jax.numpy as jnp
        import numpy as np
        B, C, D = (16, 128, 256)
        d = h_t.shape[-1]
        pre_u = jnp.einsum('bud,dk->buk', h_t, W1[:d])
        pre_v = jnp.einsum('bvd,dk->bvk', h_t, W1[d:])
        hidden = jax.nn.relu(pre_u[:, :, None, :] + pre_v[:, None, :, :] + b1)
        S = jax.nn.sigmoid(jnp.einsum('buvk,ko->buvo', hidden, W2)[..., 0] + b2[0])
        a_t = jnp.einsum('buv,bud->bvd', S * A_a, h_t)
        m_t = jnp.einsum('uv,bud->bvd', A_m, h_t) * h_t
        z_t = beta1 * h_t + beta2 * (jnp.einsum('bvd,de->bve', a_t, Wa) + ba) + beta3 * (jnp.einsum('bvd,de->bve', m_t, Wm) + bm)
        return z_t

    x = _L0_gnn_ref(x, adj, adj, L0_gnn_W1, L0_gnn_b1, L0_gnn_W2, L0_gnn_b2, L0_gnn_Wa, L0_gnn_ba, L0_gnn_Wm, L0_gnn_bm, L0_gnn_beta1, L0_gnn_beta2, L0_gnn_beta3)
    return x


_drawn_inputs = setup_inputs


def setup_inputs(seed=0):
    import zlib

    import numpy as np

    out = dict(_drawn_inputs(seed))
    spreads = {}
    factors = {'L0_gnn_b1': 8.0}
    for name, (base, spread) in spreads.items():
        noise = np.random.default_rng([zlib.crc32(name.encode()), seed]).standard_normal(out[name].shape)
        drawn = base * np.exp(spread * noise) if base else spread * noise
        out[name] = jnp.asarray(drawn.astype(out[name].dtype))
    for name, factor in factors.items():
        out[name] = (out[name] * factor).astype(out[name].dtype)
    return out
```

```python
import concourse.bass as bass
from concourse import mybir
from contextlib import ExitStack


def gnn_dense_kernel(nc, x, adj, W1, b1, W2, b2, Wa, ba, Wm, bm, beta1, beta2, beta3, out):
    fp32 = mybir.dt.float32
    ALU = mybir.AluOpType
    ACT = mybir.ActivationFunctionType

    B, N, D = x.shape
    P = 128
    NT = N // P
    DT = D // P
    HALF = 512
    NH = N // HALF
    QUAD = 32
    CT = P // QUAD
    DVE_UNITS = [(0, 0), (0, 1), (0, 2), (1, 0), (1, 1)]
    ACT_UNITS = [(0, 3), (1, 2), (1, 3)]
    LAG = 2

    ctx = ExitStack()
    with ctx:
        def sb(name, shape):
            return ctx.enter_context(nc.sbuf_tensor(name, shape, fp32))

        def sem(name):
            return ctx.enter_context(nc.semaphore(name))

        adj_sb = sb("adj_sb", [P, NT, N])
        h = sb("h", [P, NT, D])
        hT = sb("hT", [P, DT, N])
        pre_u = sb("pre_u", [P, DT, N])
        pre_v = sb("pre_v", [P, DT, N])
        gate = sb("gate", [P, NT, N])
        hid_dve = sb("hid_dve", [P, LAG, len(DVE_UNITS), N])
        hid_act = sb("hid_act", [P, LAG, len(ACT_UNITS), N])
        u_dve = sb("u_dve", [P, 2, DT, P])
        u_act = sb("u_act", [P, 2, DT, P])
        aT = sb("aT", [P, DT, N])
        mT = sb("mT", [P, DT, N])
        zb = sb("zb", [P, NT, D])
        W1_sb = sb("W1_sb", [P, 2 * DT, D])
        Wa_sb = sb("Wa_sb", [P, DT, D])
        Wm_sb = sb("Wm_sb", [P, DT, D])
        bias_row = sb("bias_row", [P, 2, D])
        b1_sb = sb("b1_sb", [P, DT])
        betas = sb("betas", [P, 4])
        ident = sb("ident", [P, P])
        w2_slide = sb("w2_slide", [P, DT, 2 * QUAD])
        logits = [ctx.enter_context(nc.psum_tensor(f"logits{i}", [P, N], fp32)) for i in range(2)]
        work = ctx.enter_context(nc.psum_tensor("work", [P, 2 * N], fp32))

        loaded = sem("loaded")
        zeroed = sem("zeroed")
        setup = sem("setup")
        h_loaded = sem("h_loaded")
        hT_psum = sem("hT_psum")
        hT_ready = sem("hT_ready")
        pre_psum = sem("pre_psum")
        pre_ready = sem("pre_ready")
        base_ready = sem("base_ready")
        u_dve_ready = sem("u_dve_ready")
        u_act_ready = sem("u_act_ready")
        hid_dve_ready = sem("hid_dve_ready")
        hid_act_ready = sem("hid_act_ready")
        hid_used = sem("hid_used")
        sigmoid_done = sem("sigmoid_done")
        gate_ready = sem("gate_ready")
        msg_m_psum = sem("msg_m_psum")
        msg_a_psum = sem("msg_a_psum")
        msg_m_ready = sem("msg_m_ready")
        msg_a_ready = sem("msg_a_ready")
        z_psum = sem("z_psum")
        z_ready = sem("z_ready")
        stored = sem("stored")
        per_batch = [h_loaded, hT_psum, hT_ready, pre_psum, pre_ready, base_ready, u_dve_ready, u_act_ready,
                     hid_dve_ready, hid_act_ready, hid_used, sigmoid_done, gate_ready,
                     msg_m_psum, msg_a_psum, msg_m_ready, msg_a_ready, z_psum, z_ready, stored]

        with nc.Block() as block:
            @block.sync
            def _(sp):
                sp.wait_ge(zeroed, 2)
                for c in range(DT):
                    sp.dma_start(w2_slide[:, c, QUAD - 1:QUAD], W2[c * P:(c + 1) * P, :]).then_inc(loaded, 16)
                    sp.dma_start(b1_sb[:, c:c + 1], b1[c * P:(c + 1) * P].rearrange("(p a) -> p a", a=1)).then_inc(loaded, 16)
                sp.dma_start(W1_sb[:], W1.rearrange("(c p) k -> p c k", p=P)).then_inc(loaded, 16)
                sp.dma_start(Wa_sb[:], Wa.rearrange("(c p) k -> p c k", p=P)).then_inc(loaded, 16)
                sp.dma_start(Wm_sb[:], Wm.rearrange("(c p) k -> p c k", p=P)).then_inc(loaded, 16)
                for i, v in enumerate((beta1, beta2, beta3, b2)):
                    sp.dma_start(betas[:, i:i + 1], v.rearrange("(a n) -> a n", a=1).broadcast_to([P, 1])).then_inc(loaded, 16)
                for i, v in enumerate((ba, bm)):
                    sp.dma_start(bias_row[:, i, :], v.rearrange("(a n) -> a n", a=1).broadcast_to([P, D])).then_inc(loaded, 16)
                sp.dma_start(adj_sb[:], adj.rearrange("(t p) v -> p t v", p=P)).then_inc(loaded, 16)
                sp.wait_ge(loaded, 16 * (2 * DT + 10))

            @block.vector
            def _(dve):
                nc.vector.memset(w2_slide[:], 0.0).then_inc(zeroed, 1)
                dve.wait_ge(loaded, 16 * (2 * DT + 10))
                nc.vector.tensor_scalar(Wa_sb[:], Wa_sb[:], betas[:, 1:2], None, ALU.mult).then_inc(setup, 1)
                nc.vector.tensor_scalar(Wm_sb[:], Wm_sb[:], betas[:, 2:3], None, ALU.mult).then_inc(setup, 1)
                nc.vector.tensor_scalar(bias_row[:, 0, :], bias_row[:, 0, :], betas[:, 1:2], None, ALU.mult).then_inc(setup, 1)
                dve.wait_ge(setup, 3)
                nc.vector.scalar_tensor_tensor(out=bias_row[:, 0, :], in0=bias_row[:, 1, :], scalar=betas[:, 2:3],
                                               in1=bias_row[:, 0, :], op0=ALU.mult, op1=ALU.add).then_inc(setup, 1)
                dve.wait_ge(setup, 4)

            @block.gpsimd
            def _(pool):
                nc.gpsimd.memset(ident[:], 0.0).then_inc(zeroed, 1)
                pool.wait_ge(zeroed, 2)
                nc.gpsimd.affine_select(out=ident[:], in_=ident[:], compare_op=ALU.not_equal, fill=1.0, base=0,
                                        pattern=[[-1, P]], channel_multiplier=1).then_inc(zeroed, 1)
                pool.wait_ge(zeroed, 3)

        with nc.Fori(0, B) as b:
            with nc.Block() as block:
                @block.sync
                def _(sp):
                    sp.dma_start(h[:], x[b, :, :].rearrange("(t p) d -> p t d", p=P)).then_inc(h_loaded, 16)
                    sp.wait_ge(z_ready, NT // 2)
                    sp.dma_start(out[b, :, :].rearrange("(t p) d -> p t d", p=P), zb[:]).then_inc(stored, 16)
                    sp.wait_ge(stored, 16)

                @block.tensor
                def _(pe):
                    pe.sem_inc(hid_used, 2 * LAG)
                    pe.wait_ge(h_loaded, 16)
                    for c in range(DT):
                        for t in range(NT):
                            last = nc.tensor.transpose(work[:, c * N + t * P:c * N + (t + 1) * P],
                                                       h[:, t, c * P:(c + 1) * P], ident[:])
                        last.then_inc(hT_psum, 1)
                    pe.wait_ge(hT_ready, DT)
                    for which in range(2):
                        for k in range(DT):
                            for n in range(NH):
                                dst = logits[k] if which == 0 else work[:, k * N:(k + 1) * N]
                                for c in range(DT):
                                    last = nc.tensor.matmul(dst[:, n * HALF:(n + 1) * HALF],
                                                            W1_sb[:, which * DT + c, k * P:(k + 1) * P],
                                                            hT[:, c, n * HALF:(n + 1) * HALF],
                                                            start=(c == 0), stop=(c == DT - 1))
                        last.then_inc(pre_psum, 1)
                    pe.wait_ge(pre_ready, 2 * DT)
                    with pe.Fori(0, NT // 2) as pair:
                        i = pair * 2
                        for par in range(2):
                            pe.wait_ge(sigmoid_done, i + par + 1)
                            for m in range(QUAD):
                                for k in range(DT):
                                    nd = sum(kk <= k for kk, _ in DVE_UNITS)
                                    na = sum(kk <= k for kk, _ in ACT_UNITS)
                                    U, V = len(DVE_UNITS), len(ACT_UNITS)
                                    pe.wait_ge(hid_dve_ready, i * (QUAD * U) + (par * QUAD + m) * U + nd)
                                    pe.wait_ge(hid_act_ready, i * (QUAD * V) + (par * QUAD + m) * V + na)
                                    for n in range(NH):
                                        for c in range(CT):
                                            if (k, c) in DVE_UNITS:
                                                src = hid_dve[:, m % LAG, DVE_UNITS.index((k, c)), :]
                                            else:
                                                src = hid_act[:, m % LAG, ACT_UNITS.index((k, c)), :]
                                            last = nc.tensor.matmul(
                                                logits[par][c * QUAD:(c + 1) * QUAD, n * HALF:(n + 1) * HALF],
                                                w2_slide[:, k, QUAD - 1 - m:2 * QUAD - 1 - m],
                                                src[:, n * HALF:(n + 1) * HALF],
                                                start=(m == 0 and k == 0), stop=(m == QUAD - 1 and k == DT - 1))
                                    last.then_inc(hid_used, 1)
                    for c in range(DT):
                        for n in range(NH):
                            for t in range(NT):
                                last = nc.tensor.matmul(work[:, c * N + n * HALF:c * N + (n + 1) * HALF],
                                                        h[:, t, c * P:(c + 1) * P], adj_sb[:, t, n * HALF:(n + 1) * HALF],
                                                        start=(t == 0), stop=(t == NT - 1))
                    last.then_inc(msg_m_psum, 1)
                    pe.wait_ge(gate_ready, NT)
                    for c in range(DT):
                        for n in range(NH):
                            for t in range(NT):
                                last = nc.tensor.matmul(logits[c][:, n * HALF:(n + 1) * HALF],
                                                        h[:, t, c * P:(c + 1) * P], gate[:, t, n * HALF:(n + 1) * HALF],
                                                        start=(t == 0), stop=(t == NT - 1))
                    last.then_inc(msg_a_psum, 1)
                    pe.wait_ge(msg_m_ready, DT)
                    pe.wait_ge(msg_a_ready, DT)
                    for t in range(NT):
                        s = 0
                        for src, w in ((mT, Wm_sb), (aT, Wa_sb)):
                            for c in range(DT):
                                last = nc.tensor.matmul(work[:, t * D:(t + 1) * D], src[:, c, t * P:(t + 1) * P],
                                                        w[:, c, :], start=(s == 0), stop=(s == 2 * DT - 1))
                                s += 1
                        if t % 2:
                            last.then_inc(z_psum, 1)

                @block.vector
                def _(dve):
                    dve.wait_ge(hT_psum, DT)
                    nc.vector.tensor_copy(hT[:, 1, :], work[:, N:2 * N]).then_inc(hT_ready, 1)
                    dve.wait_ge(pre_psum, 1)
                    nc.vector.tensor_copy(pre_u[:, 0, :], logits[0][:]).then_inc(pre_ready, 1)
                    dve.wait_ge(pre_psum, 2)
                    nc.vector.tensor_scalar(pre_v[:, 0, :], work[:, 0:N], b1_sb[:, 0:1], None, ALU.add).then_inc(pre_ready, 1)
                    dve.wait_ge(pre_ready, 2 * DT)
                    with dve.Fori(0, NT // 2) as pair:
                        i = pair * 2
                        for par in range(2):
                            nc.vector.tensor_copy(u_dve[:, par, :, :], pre_u[:].rearrange("p c (j two q) -> p c j two q", two=2, q=P)[:, :, pair, par, :]).then_inc(u_dve_ready, 1)
                            dve.wait_ge(u_dve_ready, i + par + 1)
                            for m in range(QUAD):
                                for j, (k, c) in enumerate(DVE_UNITS):
                                    if j == 0 or DVE_UNITS[j - 1][0] != k:
                                        dve.wait_ge(hid_used, i * (QUAD * DT) + (par * QUAD + m) * DT + k + 1)
                                    u = c * QUAD + m
                                    nc.vector.tensor_scalar(hid_dve[:, m % LAG, j, :], pre_v[:, k, :],
                                                            u_dve[:, par, k, u:u + 1], 0.0, ALU.add, ALU.max).then_inc(hid_dve_ready, 1)
                    dve.wait_ge(msg_m_psum, 1)
                    for c in range(DT):
                        nc.vector.tensor_tensor(mT[:, c, :], work[:, c * N:(c + 1) * N], hT[:, c, :], ALU.mult).then_inc(msg_m_ready, 1)
                    dve.wait_ge(base_ready, 2)
                    for t in range(0, NT, 2):
                        dve.wait_ge(z_psum, t // 2 + 1)
                        rows = zb[:, t:t + 2, :].rearrange("p t d -> p (t d)")
                        nc.vector.tensor_tensor(rows, rows, work[:, t * D:(t + 2) * D], ALU.add).then_inc(z_ready, 1)

                @block.scalar
                def _(act):
                    act.sem_inc(sigmoid_done, 2)
                    act.wait_ge(hT_psum, 1)
                    nc.scalar.copy(hT[:, 0, :], work[:, 0:N]).then_inc(hT_ready, 1)
                    act.wait_ge(pre_psum, 1)
                    nc.scalar.copy(pre_u[:, 1, :], logits[1][:]).then_inc(pre_ready, 1)
                    act.wait_ge(pre_psum, 2)
                    nc.scalar.activation(pre_v[:, 1, :], work[:, N:2 * N], ACT.Identity, bias=b1_sb[:, 1:2]).then_inc(pre_ready, 1)
                    act.wait_ge(pre_ready, 2 * DT)
                    with act.Fori(0, NT // 2) as pair:
                        i = pair * 2
                        for par in range(2):
                            nc.scalar.copy(u_act[:, par, :, :], pre_u[:].rearrange("p c (j two q) -> p c j two q", two=2, q=P)[:, :, pair, par, :]).then_inc(u_act_ready, 1)
                            act.wait_ge(u_act_ready, i + par + 1)
                            for m in range(QUAD):
                                for j, (k, c) in enumerate(ACT_UNITS):
                                    if j == 0 or ACT_UNITS[j - 1][0] != k:
                                        act.wait_ge(hid_used, i * (QUAD * DT) + (par * QUAD + m) * DT + k + 1)
                                    u = c * QUAD + m
                                    nc.scalar.activation(hid_act[:, m % LAG, j, :], pre_v[:, k, :], ACT.Relu,
                                                         bias=u_act[:, par, k, u:u + 1]).then_inc(hid_act_ready, 1)
                            act.wait_ge(hid_used, 2 * LAG + i * (QUAD * DT) + (par + 1) * QUAD * DT)
                            nc.scalar.activation(gate[:].rearrange("p (j two) n -> p j two n", two=2)[:, pair, par, :], logits[par][:],
                                                 ACT.Sigmoid, bias=betas[:, 3:4]).then_inc(sigmoid_done, 1)
                    for c in range(DT):
                        act.wait_ge(msg_a_psum, 1)
                        nc.scalar.copy(aT[:, c, :], logits[c][:]).then_inc(msg_a_ready, 1)

                @block.gpsimd
                def _(pool):
                    pool.wait_ge(h_loaded, 16)
                    nc.gpsimd.tensor_scalar(zb[:], h[:], betas[:, 0:1], None, ALU.mult).then_inc(base_ready, 1)
                    pool.wait_ge(base_ready, 1)
                    for t in range(NT):
                        ins = nc.gpsimd.tensor_tensor(zb[:, t, :], zb[:, t, :], bias_row[:, 0, :], ALU.add)
                    ins.then_inc(base_ready, 1)
                    with pool.Fori(0, NT) as t:
                        pool.wait_ge(sigmoid_done, t + 3)
                        g = gate[:, bass.ds(t, 1), :]
                        nc.gpsimd.tensor_tensor(g, g, adj_sb[:, bass.ds(t, 1), :], ALU.mult).then_inc(gate_ready, 1)

            nc.all_engine_barrier()
            for s in per_batch:
                nc.sync.sem_clear(s)
            nc.all_engine_barrier()


_INS = ['x', 'adj', 'L0_gnn_W1', 'L0_gnn_b1', 'L0_gnn_W2', 'L0_gnn_b2', 'L0_gnn_Wa', 'L0_gnn_ba', 'L0_gnn_Wm',
        'L0_gnn_bm', 'L0_gnn_beta1', 'L0_gnn_beta2', 'L0_gnn_beta3']
_OUTS = [((16, 1024, 256), 'float32')]


def kernel(**inputs):
    import numpy as _np
    import concourse.bacc as _bacc
    from concourse import mybir as _mybir
    from concourse.bass_utils import run_bass_kernel_spmd as _run

    nc = _bacc.Bacc("TRN2", target_bir_lowering=False, num_devices=1)
    arrays, args = {}, []
    for name in _INS:
        a = _np.asarray(inputs[name])
        a = _np.ascontiguousarray(a.reshape(1) if a.ndim == 0 else a)
        arrays[f"in_{name}_dram"] = a
        args.append(nc.dram_tensor(f"in_{name}_dram", a.shape, _mybir.dt.from_np(a.dtype), kind="ExternalInput").ap())
    for i, (shape, dtype) in enumerate(_OUTS):
        dt = _mybir.dt.from_np(_np.dtype(dtype))
        args.append(nc.dram_tensor(f"out_{i}_dram", shape, dt, kind="ExternalOutput").ap())
    gnn_dense_kernel(nc, *args)
    r = _run(nc, [arrays], core_ids=[0])
    got = tuple(r.results[0][f"out_{i}_dram"] for i in range(len(_OUTS)))
    return got[0]
```

```python
import concourse.bass as bass
from concourse import mybir
from contextlib import ExitStack


def gnn_edges_kernel(nc, x, adj, W1, b1, W2, b2, Wa, ba, Wm, bm, beta1, beta2, beta3, out):
    fp32 = mybir.dt.float32
    fp32r = mybir.dt.float32r
    i32 = mybir.dt.int32
    ALU = mybir.AluOpType
    ACT = mybir.ActivationFunctionType
    AX = mybir.AxisListType.X

    B, N, D = x.shape
    P = 128
    NT, DT = N // P, D // P
    BANK = 512
    UB, VB = 96, 32
    ST = -(-N // UB)
    NB = N // VB
    NU = ST * UB
    TILES = 2
    SLOTS = TILES * P
    PASSES = UB * VB // SLOTS
    BD = B * D
    PARTS = 2
    CH = BD // BANK
    UNITS = CH * TILES
    RING = 4
    BPC = BANK // D
    JUNK = 8

    u_rows = nc.dram_tensor("u_rows", (NU, PARTS, B, D), fp32, kind="Internal").ap()
    v_rows = nc.dram_tensor("v_rows", (N, PARTS, B, D), fp32, kind="Internal").ap()
    hWa_dram = nc.dram_tensor("hWa_dram", (B, N, D), fp32, kind="Internal").ap()
    base_dram = nc.dram_tensor("base_dram", (B, N, D), fp32, kind="Internal").ap()
    gate_dram = nc.dram_tensor("gate_dram", (B, NU, N), fp32, kind="Internal").ap()

    ctx = ExitStack()
    with ctx:
        def sb(name, shape, dt=fp32, scope=ctx):
            return scope.enter_context(nc.sbuf_tensor(name, shape, dt))

        def pb(name, shape, scope=ctx):
            return scope.enter_context(nc.psum_tensor(name, shape, fp32))

        def sem(name):
            return ctx.enter_context(nc.semaphore(name))

        def finish_step(sems):
            nc.all_engine_barrier()
            for s in sems:
                nc.sync.sem_clear(s)
            nc.all_engine_barrier()

        ident = sb("ident", [P, P])
        ones = sb("ones", [1, P])
        betas = sb("betas", [P, 4])
        w2_row = sb("w2_row", [P, D])

        loaded = sem("loaded")
        zeroed = sem("zeroed")
        setup = sem("setup")
        ident_step = sem("ident_step")

        with ExitStack() as phase:
            W1_sb = sb("W1_sb", [P, DT, 2, D], scope=phase)
            Wa_sb = sb("Wa_sb", [P, DT, D], scope=phase)
            Wm_sb = sb("Wm_sb", [P, DT, D], scope=phase)
            b1_row = sb("b1_row", [1, D], scope=phase)
            bias_row = sb("bias_row", [P, 2, D], scope=phase)
            adj_sb = sb("adj_sb", [P, NT, N], scope=phase)
            h = sb("h", [P, NT, D], scope=phase)
            hT = sb("hT", [P, DT, N], scope=phase)
            mT = sb("mT", [P, DT, N], scope=phase)
            base = sb("base", [P, NT, D], scope=phase)
            hWa = sb("hWa", [P, NT, D], scope=phase)
            split = sb("split", [P, NT, PARTS, 2, D], fp32r, scope=phase)
            zero = sb("zero", [NU - N, PARTS * BD], scope=phase)
            wide = pb("wide", [P, 4 * BANK], scope=phase)
            pairs = [pb(f"pair{i}", [P, BANK], scope=phase) for i in range(4)]

            with nc.Block() as block:
                @block.sync
                def _(sp):
                    n = 0
                    for dst, src in ((W1_sb[:, :, 0, :], W1[0:D, :].rearrange("(c p) k -> p c k", p=P)),
                                     (W1_sb[:, :, 1, :], W1[D:2 * D, :].rearrange("(c p) k -> p c k", p=P)),
                                     (Wa_sb[:], Wa.rearrange("(c p) k -> p c k", p=P)),
                                     (Wm_sb[:], Wm.rearrange("(c p) k -> p c k", p=P)),
                                     (b1_row[:], b1.rearrange("(a k) -> a k", a=1)),
                                     (w2_row[:], W2.rearrange("k a -> a k").broadcast_to([P, D])),
                                     (bias_row[:, 0, :], ba.rearrange("(a k) -> a k", a=1).broadcast_to([P, D])),
                                     (bias_row[:, 1, :], bm.rearrange("(a k) -> a k", a=1).broadcast_to([P, D])),
                                     (betas[:, 0:1], beta1.rearrange("(a k) -> a k", a=1).broadcast_to([P, 1])),
                                     (betas[:, 1:2], beta2.rearrange("(a k) -> a k", a=1).broadcast_to([P, 1])),
                                     (betas[:, 2:3], beta3.rearrange("(a k) -> a k", a=1).broadcast_to([P, 1])),
                                     (betas[:, 3:4], b2.rearrange("(a k) -> a k", a=1).broadcast_to([P, 1])),
                                     (adj_sb[:], adj.rearrange("(t p) v -> p t v", p=P))):
                        sp.dma_start(dst, src).then_inc(loaded, 16)
                        n += 16
                    sp.wait_ge(zeroed, 2)
                    sp.dma_start(u_rows[N:NU, :, :, :].rearrange("n q b k -> n (q b k)"),
                                 zero[:]).then_inc(loaded, 16)
                    sp.wait_ge(loaded, n + 16)

                @block.vector
                def _(dve):
                    nc.vector.memset(ones[:], 1.0).then_inc(zeroed, 1)
                    nc.vector.memset(zero[:], 0.0).then_inc(zeroed, 1)
                    dve.wait_ge(loaded, 14 * 16)
                    nc.vector.tensor_scalar(Wa_sb[:], Wa_sb[:], betas[:, 1:2], None, ALU.mult).then_inc(setup, 1)
                    nc.vector.tensor_scalar(Wm_sb[:], Wm_sb[:], betas[:, 2:3], None, ALU.mult).then_inc(setup, 1)
                    nc.vector.tensor_scalar(bias_row[:, 0, :], bias_row[:, 0, :], betas[:, 1:2], None,
                                            ALU.mult).then_inc(setup, 1)
                    dve.wait_ge(setup, 3)
                    nc.vector.scalar_tensor_tensor(out=bias_row[:, 0, :], in0=bias_row[:, 1, :], scalar=betas[:, 2:3],
                                                   in1=bias_row[:, 0, :], op0=ALU.mult, op1=ALU.add).then_inc(setup, 1)
                    dve.wait_ge(setup, 4)

                @block.gpsimd
                def _(pool):
                    nc.gpsimd.memset(ident[:], 0.0).then_inc(ident_step, 1)
                    pool.wait_ge(ident_step, 1)
                    nc.gpsimd.affine_select(out=ident[:], in_=ident[:], compare_op=ALU.not_equal, fill=1.0, base=0,
                                            pattern=[[-1, P]], channel_multiplier=1).then_inc(ident_step, 1)
                    pool.wait_ge(ident_step, 2)

            h_loaded = sem("h_loaded")
            hT_psum = sem("hT_psum")
            hT_ready = sem("hT_ready")
            pre_psum = sem("pre_psum")
            high_ready = sem("high_ready")
            split_ready = sem("split_ready")
            hWa_psum = sem("hWa_psum")
            hWa_ready = sem("hWa_ready")
            msg_psum = sem("msg_psum")
            msg_ready = sem("msg_ready")
            scaled = sem("scaled")
            base_psum = sem("base_psum")
            base_ready = sem("base_ready")
            stored = sem("stored")
            node_sems = [h_loaded, hT_psum, hT_ready, pre_psum, high_ready, split_ready, hWa_psum, hWa_ready,
                         msg_psum, msg_ready, scaled, base_psum, base_ready, stored]

            with nc.Fori(0, B) as b:
                with nc.Block() as block:
                    @block.sync
                    def _(sp):
                        sp.dma_start(h[:], x[b, :, :].rearrange("(t p) d -> p t d", p=P)).then_inc(h_loaded, 16)
                        sp.wait_ge(split_ready, NT)
                        for w, rows in ((0, u_rows), (1, v_rows)):
                            for q in range(PARTS):
                                sp.dma_start(rows[0:N, q, b, :].rearrange("(t p) k -> p t k", p=P),
                                             split[:, :, q, w, :].bitcast(fp32)).then_inc(stored, 16)
                        sp.wait_ge(hWa_ready, NT // 2)
                        sp.dma_start(hWa_dram[b, :, :].rearrange("(t p) d -> p t d", p=P), hWa[:]).then_inc(stored, 16)
                        sp.wait_ge(base_ready, NT // 2)
                        sp.dma_start(base_dram[b, :, :].rearrange("(t p) d -> p t d", p=P), base[:]).then_inc(stored, 16)
                        sp.wait_ge(stored, (2 * PARTS + 2) * 16)

                    @block.tensor
                    def _(pe):
                        pe.wait_ge(h_loaded, 16)
                        for c in range(DT):
                            for t in range(NT):
                                last = nc.tensor.transpose(wide[:, c * N + t * P:c * N + (t + 1) * P],
                                                           h[:, t, c * P:(c + 1) * P], ident[:])
                            last.then_inc(hT_psum, 1)
                        pe.wait_ge(hT_ready, DT)
                        for t in range(NT):
                            if t >= 4:
                                pe.wait_ge(split_ready, t - 3)
                            bank = pairs[t % 4]
                            for c in range(DT):
                                nc.tensor.matmul(bank[:], hT[:, c, t * P:(t + 1) * P],
                                                 W1_sb[:, c, :, :].rearrange("p w k -> p (w k)"),
                                                 start=(c == 0), stop=False)
                            nc.tensor.matmul(bank[:, D:2 * D], ones[0:1, :], b1_row[0:1, :],
                                             start=False, stop=True).then_inc(pre_psum, 1)
                        for c in range(DT):
                            for n in range(N // BANK):
                                for t in range(NT):
                                    last = nc.tensor.matmul(wide[:, c * N + n * BANK:c * N + (n + 1) * BANK],
                                                            h[:, t, c * P:(c + 1) * P],
                                                            adj_sb[:, t, n * BANK:(n + 1) * BANK],
                                                            start=(t == 0), stop=(t == NT - 1))
                        last.then_inc(msg_psum, 1)
                        for t in range(NT):
                            if t % 2 == 0:
                                pe.wait_ge(split_ready, NT // 2 + t // 2 + 1)
                            for c in range(DT):
                                last = nc.tensor.matmul(pairs[t // 2][:, (t % 2) * D:(t % 2 + 1) * D],
                                                        hT[:, c, t * P:(t + 1) * P], Wa_sb[:, c, :],
                                                        start=(c == 0), stop=(c == DT - 1))
                            if t % 2:
                                last.then_inc(hWa_psum, 1)
                        pe.wait_ge(msg_ready, DT)
                        for t in range(NT):
                            if t % 2 == 0:
                                pe.wait_ge(hWa_ready, t // 2 + 1)
                            for c in range(DT):
                                last = nc.tensor.matmul(pairs[t // 2][:, (t % 2) * D:(t % 2 + 1) * D],
                                                        mT[:, c, t * P:(t + 1) * P], Wm_sb[:, c, :],
                                                        start=(c == 0), stop=(c == DT - 1))
                            if t % 2:
                                last.then_inc(base_psum, 1)

                    @block.scalar
                    def _(act):
                        act.wait_ge(hT_psum, 1)
                        nc.scalar.copy(hT[:, 0, :], wide[:, 0:N]).then_inc(hT_ready, 1)
                        for t in range(NT):
                            act.wait_ge(pre_psum, t + 1)
                            nc.scalar.copy(split[:, t, 0, :, :].rearrange("p w k -> p (w k)"),
                                           pairs[t % 4][:]).then_inc(high_ready, 1)
                        for t in range(NT // 2):
                            act.wait_ge(hWa_psum, t + 1)
                            nc.scalar.copy(hWa[:, 2 * t:2 * t + 2, :].rearrange("p t k -> p (t k)"),
                                           pairs[t][:]).then_inc(hWa_ready, 1)

                    @block.vector
                    def _(dve):
                        dve.wait_ge(hT_psum, 2)
                        nc.vector.tensor_copy(hT[:, 1, :], wide[:, N:2 * N]).then_inc(hT_ready, 1)
                        for t in range(NT):
                            dve.wait_ge(high_ready, t + 1)
                            nc.vector.tensor_tensor(split[:, t, 1, :, :].rearrange("p w k -> p (w k)"), pairs[t % 4][:],
                                                    split[:, t, 0, :, :].rearrange("p w k -> p (w k)").bitcast(fp32),
                                                    ALU.subtract).then_inc(split_ready, 1)
                        dve.wait_ge(msg_psum, 1)
                        for c in range(DT):
                            nc.vector.tensor_tensor(mT[:, c, :], wide[:, c * N:(c + 1) * N], hT[:, c, :],
                                                    ALU.mult).then_inc(msg_ready, 1)
                        dve.wait_ge(scaled, 2)
                        for t in range(NT // 2):
                            dve.wait_ge(base_psum, t + 1)
                            rows = base[:, 2 * t:2 * t + 2, :].rearrange("p t k -> p (t k)")
                            nc.vector.tensor_tensor(rows, rows, pairs[t][:], ALU.add).then_inc(base_ready, 1)

                    @block.gpsimd
                    def _(pool):
                        pool.wait_ge(h_loaded, 16)
                        nc.gpsimd.tensor_scalar(base[:], h[:], betas[:, 0:1], None, ALU.mult).then_inc(scaled, 1)
                        pool.wait_ge(scaled, 1)
                        nc.gpsimd.tensor_tensor(base[:], base[:],
                                                bias_row[:, 0, :].rearrange("p (a k) -> p a k", a=1).broadcast_to([P, NT, D]),
                                                ALU.add).then_inc(scaled, 1)
                finish_step(node_sems)

        edges = ctx.enter_context(ExitStack())
        adj_u = sb("adj_u", [UB, ST, N], scope=edges)
        rank_end = sb("rank_end", [UB, ST * N + VB], scope=edges)
        row_start = sb("row_start", [UB, ST * NB + 1], scope=edges)
        row_end = sb("row_end", [UB, ST * NB + 1], scope=edges)
        slot_row = sb("slot_row", [UB, SLOTS], scope=edges)
        slot_col = sb("slot_col", [P, TILES, VB], scope=edges)
        passes_i = sb("passes_i", [1, 1], i32, scope=edges)

        with ExitStack() as phase:
            is_edge = sb("is_edge", [UB, ST * N], scope=phase)
            restart = sb("restart", [UB, N], scope=phase)
            above = sb("above", [UB, UB], scope=phase)
            counts = sb("counts", [UB, ST * NB], scope=phase)
            ones_col = sb("ones_col", [UB, 1], scope=phase)
            full = sb("full", [1, 4], scope=phase)
            levels = sb("levels", [1, PASSES], scope=phase)
            over = sb("over", [1, PASSES], scope=phase)
            start_psum = pb("start_psum", [UB, BANK], scope=phase)
            total_psum = pb("total_psum", [1, BANK], scope=phase)
            a_loaded = sem("a_loaded")
            a_zero = sem("a_zero")
            consts = sem("consts")
            step = sem("step")
            counted = sem("counted")
            summed = sem("summed")
            with nc.Block() as block:
                @block.sync
                def _(sp):
                    whole = N // UB
                    sp.dma_start(adj_u[:, 0:whole, :],
                                 adj[0:whole * UB, :].rearrange("(s p) v -> p s v", p=UB)).then_inc(a_loaded, 16)
                    sp.wait_ge(a_zero, 1)
                    sp.dma_start(adj_u[0:N - whole * UB, whole, :], adj[whole * UB:N, :]).then_inc(a_loaded, 16)
                    sp.wait_ge(a_loaded, 32)

                @block.gpsimd
                def _(pool):
                    nc.gpsimd.memset(above[:], 0.0).then_inc(consts, 1)
                    pool.wait_ge(consts, 1)
                    nc.gpsimd.affine_select(out=above[:], in_=above[:], compare_op=ALU.is_ge, fill=1.0, base=0,
                                            pattern=[[-1, UB]], channel_multiplier=1).then_inc(consts, 1)
                    nc.gpsimd.iota(slot_row[:], pattern=[[1, SLOTS]], base=0, channel_multiplier=0,
                                   allow_small_or_imprecise_dtypes=True).then_inc(consts, 1)
                    nc.gpsimd.iota(slot_col[:], pattern=[[P, TILES], [0, VB]], base=1, channel_multiplier=1,
                                   allow_small_or_imprecise_dtypes=True).then_inc(consts, 1)
                    nc.gpsimd.iota(levels[:], pattern=[[SLOTS, PASSES]], base=0, channel_multiplier=0,
                                   allow_small_or_imprecise_dtypes=True).then_inc(consts, 1)

                @block.vector
                def _(dve):
                    done = [0]

                    def link(ins):
                        done[0] += 1
                        ins.then_inc(step, 1)
                        dve.wait_ge(step, done[0])

                    nc.vector.memset(adj_u[:, ST - 1, :], 0.0).then_inc(a_zero, 1)
                    link(nc.vector.memset(restart[:], 1.0))
                    link(nc.vector.memset(restart[:].rearrange("p (n w) -> p n w", w=VB)[:, :, 0:1], 0.0))
                    link(nc.vector.memset(ones_col[:], 1.0))
                    link(nc.vector.memset(rank_end[:, ST * N:], 0.0))
                    link(nc.vector.memset(row_start[:, ST * NB:], 0.0))
                    link(nc.vector.memset(row_end[:, ST * NB:], 0.0))
                    dve.wait_ge(a_loaded, 32)
                    link(nc.vector.tensor_scalar(is_edge[:], adj_u[:].rearrange("p s v -> p (s v)"), 0.0, None, ALU.not_equal))
                    for s in range(ST):
                        link(nc.vector.tensor_tensor_scan(rank_end[:, s * N:(s + 1) * N], restart[:],
                                                          is_edge[:, s * N:(s + 1) * N], 0.0, ALU.mult, ALU.add))
                    link(nc.vector.tensor_copy(counts[:], rank_end[:, 0:ST * N].rearrange("p (n w) -> p n w", w=VB)[:, :, VB - 1]))
                    nc.vector.memset(full[:], 0.0).then_inc(counted, 1)
                    link(nc.vector.tensor_tensor(rank_end[:, 0:ST * N], rank_end[:, 0:ST * N], is_edge[:], ALU.mult))
                    dve.wait_ge(summed, 1)
                    link(nc.vector.tensor_copy(row_start[:, 0:ST * NB], start_psum[:, 0:ST * NB]))
                    link(nc.vector.tensor_tensor(row_end[:, 0:ST * NB], row_start[:, 0:ST * NB], counts[:], ALU.add))
                    blocks = rank_end[:, 0:ST * N].rearrange("p (n w) -> p n w", w=VB)
                    link(nc.vector.tensor_tensor(blocks, blocks,
                                                 row_start[:, 0:ST * NB].rearrange("p (n a) -> p n a", a=1).broadcast_to([UB, ST * NB, VB]),
                                                 ALU.add))
                    link(nc.vector.tensor_reduce(full[:, 0:1], total_psum[0:1, 0:ST * NB], AX, ALU.max))
                    dve.wait_ge(consts, 5)
                    link(nc.vector.tensor_scalar(over[:], levels[:], full[:, 0:1], None, ALU.is_lt))
                    link(nc.vector.tensor_reduce(full[:, 1:2], over[:], AX, ALU.add))
                    link(nc.vector.tensor_copy(passes_i[:], full[:, 1:2]))

                @block.tensor
                def _(pe):
                    pe.wait_ge(counted, 1)
                    pe.wait_ge(consts, 2)
                    nc.tensor.matmul(start_psum[:, 0:ST * NB], above[:], counts[:], start=True, stop=True)
                    nc.tensor.matmul(total_psum[0:1, 0:ST * NB], ones_col[:], counts[:], start=True, stop=True).then_inc(summed, 1)

        passes = nc.values_load(passes_i[0:1, 0:1], min_val=0, max_val=PASSES)

        rows = [sb(f"rows{i}", [P, PARTS, BD], fp32r, scope=edges) for i in range(2)]
        pick = [sb(f"pick{i}", [P, SLOTS], fp32r, scope=edges) for i in range(2)]
        ge_start = sb("ge_start", [UB, SLOTS], scope=edges)
        u_of_slot = [sb(f"u_of_slot{i}", [P, TILES, UB], scope=edges) for i in range(2)]
        v_of_slot = [sb(f"v_of_slot{i}", [P, TILES, VB], scope=edges) for i in range(2)]
        junk = sb("junk", [P, JUNK, D], scope=edges)
        score = [sb(f"score{i}", [P, TILES, B], scope=edges) for i in range(2)]
        gate = [sb(f"gate{i}", [P, TILES, B], scope=edges) for i in range(2)]
        spread = [sb(f"spread{i}", [P, TILES, B, VB], scope=edges) for i in range(2)]
        placed = [sb(f"placed{i}", [UB, B, VB], scope=edges) for i in range(2)]
        gated = sb("gated", [UB, B, 2 * VB], scope=edges)
        earlier = sb("earlier", [UB, B, 2 * VB], scope=edges)
        with ExitStack() as phase:
            gather = [pb(f"gather{i}", [P, BANK], scope=phase) for i in range(RING)]
            rank_psum = pb("rank_psum", [P, BANK], scope=phase)
            flip_psum = pb("flip_psum", [P, BANK], scope=phase)
            place_psum = [pb(f"place_psum{i}", [UB, BANK], scope=phase) for i in range(2)]

            rows_loaded = [sem("rows_loaded0"), sem("rows_loaded1")]
            pick_u_part = sem("pick_u_part")
            pick_u = sem("pick_u")
            ranked = sem("ranked")
            v_picked = sem("v_picked")
            flipped = sem("flipped")
            picks_ready = sem("picks_ready")
            gathered = sem("gathered")
            scored = sem("scored")
            gated_slots = sem("gated_slots")
            spread_ready = sem("spread_ready")
            placed_psum = sem("placed_psum")
            placed_ready = sem("placed_ready")
            masked = sem("masked")
            gate_stored = sem("gate_stored")
            earlier_loaded = sem("earlier_loaded")
            merged = sem("merged")
            edge_sems = [*rows_loaded, pick_u_part, pick_u, ranked, v_picked, flipped, picks_ready, gathered, scored,
                         gated_slots, spread_ready, placed_psum, placed_ready, masked, gate_stored,
                         earlier_loaded, merged]

            def strip(s, first):
                with nc.Block() as block:
                    def waits(eng, sem_, value):
                        if not isinstance(value, int) or value > 0:
                            eng.wait_ge(sem_, value)

                    def load_v(sp, n, par):
                        for q in range(PARTS):
                            sp.dma_start(rows[par][UB:P, q, :].bitcast(fp32),
                                         v_rows[bass.ds(n * VB, VB), q, :, :].rearrange("n b k -> n (b k)")).then_inc(rows_loaded[par], 16)

                    def store(sp, j):
                        place_ = gate_dram[:, bass.ds(s * UB, UB), bass.ds(j * 2 * VB, 2 * VB)].rearrange("b u v -> u b v")
                        waits(sp, masked, (j + 1) * 2)
                        if not first:
                            sp.dma_start(earlier[:], place_).then_inc(earlier_loaded, 16)
                            waits(sp, merged, j + 1)
                        sp.dma_start(place_, gated[:]).then_inc(gate_stored, 16)

                    @block.sync
                    def _(sp):
                        for par in range(2):
                            for q in range(PARTS):
                                sp.dma_start(rows[par][0:UB, q, :].bitcast(fp32),
                                             u_rows[bass.ds(s * UB, UB), q, :, :].rearrange("n b k -> n (b k)")).then_inc(rows_loaded[par], 16)
                            load_v(sp, par, par)
                        for par in range(2):
                            sp.wait_ge(gathered, UNITS * (par + 1))
                            load_v(sp, par + 2, par)
                        with sp.Fori(1, NB // 2 - 1) as j:
                            for par in range(2):
                                sp.wait_ge(gathered, j * (2 * UNITS) + UNITS * (par + 1))
                                load_v(sp, j * 2 + (2 + par), par)
                                if par == 0:
                                    store(sp, j - 1)
                        for j in (NB // 2 - 2, NB // 2 - 1):
                            store(sp, j)
                        sp.wait_ge(gate_stored, 16 * (NB // 2))

                    @block.tensor
                    def _(pe):
                        def rank(n, par):
                            waits(pe, pick_u, n + 1)
                            waits(pe, v_picked, n)
                            for t in range(TILES):
                                last = nc.tensor.matmul(rank_psum[:, t * VB:(t + 1) * VB],
                                                        pick[par][0:UB, t * P:(t + 1) * P].bitcast(fp32),
                                                        rank_end[:, bass.ds(s * N + n * VB, VB)], start=True, stop=True)
                            last.then_inc(ranked, 1)

                        def flip(n, par):
                            waits(pe, v_picked, n + 1)
                            waits(pe, picks_ready, 2 * n)
                            for t in range(TILES):
                                nc.tensor.transpose(flip_psum[:, t * UB:(t + 1) * UB],
                                                    pick[par][0:UB, t * P:(t + 1) * P].bitcast(fp32), ident[0:UB, 0:UB])
                            for t in range(TILES):
                                last = nc.tensor.matmul(flip_psum[UB:P, 2 * UB + t * P:2 * UB + (t + 1) * P],
                                                        v_of_slot[par][:, t, :], ident[:], start=True, stop=True)
                            last.then_inc(flipped, 1)

                        def place(n, par):
                            waits(pe, spread_ready, TILES * (n + 1))
                            waits(pe, placed_ready, n - 1 if isinstance(n, int) else n + (-1))
                            for t in range(TILES):
                                last = nc.tensor.matmul(place_psum[par][:], u_of_slot[par][:, t, :],
                                                        spread[par][:, t, :, :].rearrange("p b v -> p (b v)"),
                                                        start=(t == 0), stop=(t == TILES - 1))
                            last.then_inc(placed_psum, 1)

                        def one(n, j, par, prev, prev_n):
                            waits(pe, rows_loaded[par], 16 * PARTS * (j + 2))
                            waits(pe, picks_ready, 2 * (n + 1))
                            for c in range(CH):
                                for t in range(TILES):
                                    unit = c * TILES + t
                                    if unit == 6:
                                        rank(n + 1, 1 - par)
                                    if unit == 10 and prev:
                                        place(prev_n, 1 - par)
                                    if unit == 13:
                                        flip(n + 1, 1 - par)
                                    if not isinstance(n, int) or n * UNITS + unit >= RING:
                                        waits(pe, scored, n * UNITS + (unit - RING + 1))
                                    for q in range(PARTS):
                                        last = nc.tensor.matmul(gather[unit % RING][:], pick[par][:, t * P:(t + 1) * P],
                                                                rows[par][:, q, c * BANK:(c + 1) * BANK],
                                                                start=(q == 0), stop=(q == PARTS - 1))
                                    last.then_inc(gathered, 1)

                        rank(0, 0)
                        flip(0, 0)
                        one(0, 0, 0, False, 0)
                        one(1, 0, 1, True, 0)
                        with pe.Fori(1, NB // 2) as j:
                            one(j * 2, j, 0, True, j * 2 + (-1))
                            one(j * 2 + 1, j, 1, True, j * 2)
                        place(NB - 1, 1)

                    @block.vector
                    def _(dve):
                        def pick_rows(n, par):
                            col = s * NB + n
                            waits(dve, gathered, n * UNITS + (-UNITS))
                            nc.vector.tensor_scalar(ge_start[:], slot_row[:], row_start[:, bass.ds(col, 1)], None,
                                                    ALU.is_ge).then_inc(pick_u_part, 1)
                            waits(dve, pick_u_part, n + 1)
                            nc.vector.scalar_tensor_tensor(out=pick[par][0:UB, :], in0=slot_row[:],
                                                           scalar=row_end[:, bass.ds(col, 1)], in1=ge_start[:],
                                                           op0=ALU.is_lt, op1=ALU.mult).then_inc(pick_u, 1)

                        def pick_columns(n, par):
                            waits(dve, ranked, n + 1)
                            waits(dve, spread_ready, n * TILES + (-TILES))
                            nc.vector.tensor_tensor(v_of_slot[par][:], rank_psum[:, 0:TILES * VB].rearrange("p (t v) -> p t v", t=TILES),
                                                    slot_col[:], ALU.is_equal).then_inc(v_picked, 1)

                        def one(n, par):
                            pick_rows(n + 1, 1 - par)
                            waits(dve, gated_slots, n + (-1))
                            for c in range(CH):
                                for t in range(TILES):
                                    unit = c * TILES + t
                                    waits(dve, gathered, n * UNITS + (unit + 1))
                                    for i in range(BPC):
                                        b_ = c * BPC + i
                                        slot = (unit * BPC + i) % JUNK
                                        if i == 0 and unit % 2 == 0:
                                            waits(dve, scored, n * UNITS + (unit - 2))
                                        ins = nc.vector.scalar_tensor_tensor(
                                            out=junk[:, slot, :], in0=gather[unit % RING][:, i * D:(i + 1) * D], scalar=0.0,
                                            in1=w2_row[:], op0=ALU.max, op1=ALU.mult, accum_out=score[par][:, t, b_:b_ + 1])
                                    ins.then_inc(scored, 1)
                                    if unit == 10:
                                        pick_columns(n + 1, 1 - par)

                        pick_rows(0, 0)
                        pick_columns(0, 0)
                        one(0, 0)
                        one(1, 1)
                        with dve.Fori(1, NB // 2) as j:
                            one(j * 2, 0)
                            one(j * 2 + 1, 1)

                    @block.scalar
                    def _(act):
                        def sigmoid(n, par):
                            waits(act, scored, (n + 1) * UNITS)
                            waits(act, spread_ready, n * TILES + (-TILES))
                            nc.scalar.activation(gate[par][:], score[par][:], ACT.Sigmoid, bias=betas[:, 3:4]).then_inc(gated_slots, 1)

                        def take_placed(n, par):
                            waits(act, placed_psum, n + 1)
                            waits(act, masked, n + (-1))
                            nc.scalar.copy(placed[par][:].rearrange("p b v -> p (b v)"), place_psum[par][:]).then_inc(placed_ready, 1)

                        def take_picks(n, par):
                            waits(act, flipped, n + 1)
                            waits(act, placed_psum, n + (-1))
                            nc.scalar.copy(u_of_slot[par][:].rearrange("p t u -> p (t u)"), flip_psum[:, 0:TILES * UB]).then_inc(picks_ready, 1)
                            nc.scalar.copy(pick[par][UB:P, :], flip_psum[UB:P, 2 * UB:2 * UB + SLOTS]).then_inc(picks_ready, 1)

                        def one(n, par, prev, prev_n):
                            if prev:
                                sigmoid(prev_n, 1 - par)
                                take_placed(prev_n, 1 - par)
                            take_picks(n + 1, 1 - par)

                        take_picks(0, 0)
                        one(0, 0, False, 0)
                        one(1, 1, True, 0)
                        with act.Fori(1, NB // 2) as j:
                            one(j * 2, 0, True, j * 2 + (-1))
                            one(j * 2 + 1, 1, True, j * 2)
                        sigmoid(NB - 1, 1)
                        take_placed(NB - 1, 1)

                    @block.gpsimd
                    def _(pool):
                        def spread_gates(n, par):
                            waits(pool, gated_slots, n + 1)
                            waits(pool, placed_psum, n + (-1))
                            for t in range(TILES):
                                nc.gpsimd.tensor_tensor(
                                    spread[par][:, t, :, :],
                                    v_of_slot[par][:, t, :].rearrange("p (a v) -> p a v", a=1).broadcast_to([P, B, VB]),
                                    gate[par][:, t, :].rearrange("p (b a) -> p b a", a=1).broadcast_to([P, B, VB]),
                                    ALU.mult).then_inc(spread_ready, 1)

                        def mask(n, j, par):
                            waits(pool, placed_ready, n + 1)
                            if par == 0:
                                waits(pool, gate_stored, 16 * j)
                            nc.gpsimd.tensor_tensor(
                                gated[:, :, par * VB:(par + 1) * VB], placed[par][:],
                                adj_u[:].rearrange("p s v -> p (s v)")[:, bass.ds(s * N + n * VB, VB)]
                                .rearrange("p (a v) -> p a v", a=1).broadcast_to([UB, B, VB]),
                                ALU.mult).then_inc(masked, 1)
                            if par == 1 and not first:
                                waits(pool, masked, n + 1)
                                waits(pool, earlier_loaded, 16 * (j + 1))
                                nc.gpsimd.tensor_tensor(gated[:], gated[:], earlier[:], ALU.add).then_inc(merged, 1)

                        spread_gates(0, 0)
                        mask(0, 0, 0)
                        with pool.Fori(1, NB // 2) as j:
                            spread_gates(j * 2 + (-1), 1)
                            mask(j * 2 + (-1), j - 1, 1)
                            spread_gates(j * 2, 0)
                            mask(j * 2, j, 0)
                        spread_gates(NB - 1, 1)
                        mask(NB - 1, NB // 2 - 1, 1)
                finish_step(edge_sems)

            with nc.Fori(0, ST) as s:
                strip(s, True)
            shifted = sem("shifted")
            with nc.If(passes > 1):
                with nc.Fori(1, passes):
                    with nc.Block() as block:
                        @block.vector
                        def _(dve):
                            nc.vector.tensor_scalar(slot_row[:], slot_row[:], float(SLOTS), None, ALU.add).then_inc(shifted, 1)
                            nc.vector.tensor_scalar(slot_col[:], slot_col[:], float(SLOTS), None, ALU.add).then_inc(shifted, 1)
                            dve.wait_ge(shifted, 2)
                    finish_step([shifted])
                    with nc.Fori(0, ST) as s:
                        strip(s, False)
                    finish_step([shifted])
        edges.close()

        with ExitStack() as phase:
            gate_b = sb("gate_b", [P, NT, N], scope=phase)
            hWa_b = sb("hWa_b", [P, NT, D], scope=phase)
            z = sb("z", [P, NT, D], scope=phase)
            z_psum = [pb(f"z_psum{i}", [P, BANK], scope=phase) for i in range(4)]
            gate_loaded = [sem(f"gate_loaded{i}") for i in range(NT)]
            hWa_loaded = sem("hWa_loaded")
            z_loaded = sem("z_loaded")
            z_summed = sem("z_summed")
            z_ready = sem("z_ready")
            z_stored = sem("z_stored")
            with nc.Fori(0, B) as b:
                with nc.Block() as block:
                    @block.sync
                    def _(sp):
                        sp.dma_start(hWa_b[:], hWa_dram[b, :, :].rearrange("(t p) d -> p t d", p=P)).then_inc(hWa_loaded, 16)
                        for t in range(NT):
                            sp.dma_start(gate_b[:, t, :], gate_dram[b, t * P:(t + 1) * P, :]).then_inc(gate_loaded[t], 16)
                        sp.dma_start(z[:], base_dram[b, :, :].rearrange("(t p) d -> p t d", p=P)).then_inc(z_loaded, 16)
                        sp.wait_ge(z_ready, NT // 2)
                        sp.dma_start(out[b, :, :].rearrange("(t p) d -> p t d", p=P), z[:]).then_inc(z_stored, 16)
                        sp.wait_ge(z_stored, 16)

                    @block.tensor
                    def _(pe):
                        pe.wait_ge(hWa_loaded, 16)
                        for v in range(NT):
                            for t in range(NT):
                                pe.wait_ge(gate_loaded[t], 16)
                                last = nc.tensor.matmul(z_psum[v // 2][:, (v % 2) * D:(v % 2 + 1) * D],
                                                        gate_b[:, t, v * P:(v + 1) * P], hWa_b[:, t, :],
                                                        start=(t == 0), stop=(t == NT - 1))
                            if v % 2:
                                last.then_inc(z_summed, 1)

                    @block.vector
                    def _(dve):
                        dve.wait_ge(z_loaded, 16)
                        for t in range(NT // 2):
                            dve.wait_ge(z_summed, t + 1)
                            rows_ = z[:, 2 * t:2 * t + 2, :].rearrange("p t k -> p (t k)")
                            nc.vector.tensor_tensor(rows_, rows_, z_psum[t][:], ALU.add).then_inc(z_ready, 1)
                finish_step([*gate_loaded, hWa_loaded, z_loaded, z_summed, z_ready, z_stored])


_INS = ['x', 'adj', 'L0_gnn_W1', 'L0_gnn_b1', 'L0_gnn_W2', 'L0_gnn_b2', 'L0_gnn_Wa', 'L0_gnn_ba', 'L0_gnn_Wm',
        'L0_gnn_bm', 'L0_gnn_beta1', 'L0_gnn_beta2', 'L0_gnn_beta3']
_OUTS = [((16, 1024, 256), 'float32')]


def kernel(**inputs):
    import numpy as _np
    import concourse.bacc as _bacc
    from concourse import mybir as _mybir
    from concourse.bass_utils import run_bass_kernel_spmd as _run

    nc = _bacc.Bacc("TRN2", target_bir_lowering=False, num_devices=1)
    arrays, args = {}, []
    for name in _INS:
        a = _np.asarray(inputs[name])
        a = _np.ascontiguousarray(a.reshape(1) if a.ndim == 0 else a)
        arrays[f"in_{name}_dram"] = a
        args.append(nc.dram_tensor(f"in_{name}_dram", a.shape, _mybir.dt.from_np(a.dtype), kind="ExternalInput").ap())
    for i, (shape, dtype) in enumerate(_OUTS):
        dt = _mybir.dt.from_np(_np.dtype(dtype))
        args.append(nc.dram_tensor(f"out_{i}_dram", shape, dt, kind="ExternalOutput").ap())
    gnn_edges_kernel(nc, *args)
    r = _run(nc, [arrays], core_ids=[0])
    got = tuple(r.results[0][f"out_{i}_dram"] for i in range(len(_OUTS)))
    return got[0]
```

```python
import concourse.bass as bass
from concourse import mybir
from contextlib import ExitStack


def gnn_edges_kernel(nc, x, adj, W1, b1, W2, b2, Wa, ba, Wm, bm, beta1, beta2, beta3, out):
    fp32 = mybir.dt.float32
    fp32r = mybir.dt.float32r
    i32 = mybir.dt.int32
    ALU = mybir.AluOpType
    ACT = mybir.ActivationFunctionType
    AX = mybir.AxisListType.X

    B, N, D = x.shape
    P = 128
    NT, DT = N // P, D // P
    BANK = 512
    UB, VB = 96, 32
    ST = -(-N // UB)
    NB = N // VB
    NU = ST * UB
    TILES = 2
    SLOTS = TILES * P
    PASSES = UB * VB // SLOTS
    BD = B * D
    PARTS = 2
    HD = D // 2
    BPC = BANK // HD
    CH = B // BPC
    UNITS = [(c, half, t) for c in range(CH) for t in range(TILES) for half in range(2)]
    OWNER = ["dve" if half == 0 or (c, t) == (CH - 1, TILES - 1) else "act" for c, half, t in UNITS]
    N_OF = {e: OWNER.count(e) for e in ("dve", "act")}
    RING = {"dve": 3, "act": 2}
    LAST = OWNER[-1]
    TURNS = 4
    AHEAD = 2
    assert N_OF["dve"] % RING["dve"] == 0 and 2 * N_OF["act"] % RING["act"] == 0

    u_rows = nc.dram_tensor("u_rows", (NU, PARTS, B, D), fp32, kind="Internal").ap()
    v_rows = nc.dram_tensor("v_rows", (N, PARTS, B, D), fp32, kind="Internal").ap()
    hWa_dram = nc.dram_tensor("hWa_dram", (B, N, D), fp32, kind="Internal").ap()
    base_dram = nc.dram_tensor("base_dram", (B, N, D), fp32, kind="Internal").ap()
    gate_dram = nc.dram_tensor("gate_dram", (B, NU, N), fp32, kind="Internal").ap()

    ctx = ExitStack()
    with ctx:
        def sb(name, shape, dt=fp32, scope=ctx):
            return scope.enter_context(nc.sbuf_tensor(name, shape, dt))

        def pb(name, shape, scope=ctx):
            return scope.enter_context(nc.psum_tensor(name, shape, fp32))

        def sem(name):
            return ctx.enter_context(nc.semaphore(name))

        def waits(eng, sem_, value):
            if not isinstance(value, int) or value > 0:
                eng.wait_ge(sem_, value)

        def each_batch(eng, one):
            for par in range(2):
                one(par, 0, par)
            with eng.Fori(1, B // 2) as j:
                for par in range(2):
                    one(j * 2 + par, j, par)

        def finish_step(sems):
            nc.all_engine_barrier()
            for s in sems:
                nc.sync.sem_clear(s)
            nc.all_engine_barrier()

        ident = sb("ident", [P, P])
        ones = sb("ones", [1, P])
        betas = sb("betas", [P, 4])
        w2_row = sb("w2_row", [P, HD])
        sign = sb("sign", [P, 1])

        loaded = sem("loaded")
        zeroed = sem("zeroed")
        setup = sem("setup")
        ident_step = sem("ident_step")

        with ExitStack() as phase:
            W1_sb = sb("W1_sb", [P, DT, 2, D], scope=phase)
            Wa_sb = sb("Wa_sb", [P, DT, D], scope=phase)
            Wm_sb = sb("Wm_sb", [P, DT, D], scope=phase)
            b1_row = sb("b1_row", [1, D], scope=phase)
            bias_row = sb("bias_row", [P, 2, D], scope=phase)
            w2_all = sb("w2_all", [P, D], scope=phase)
            w2_col = sb("w2_col", [P, DT], scope=phase)
            b1_col = sb("b1_col", [P, DT], scope=phase)
            adj_sb = sb("adj_sb", [P, NT, N], scope=phase)
            h = [sb(f"h{i}", [P, NT, D], scope=phase) for i in range(2)]
            hT = sb("hT", [P, DT, N], scope=phase)
            mT = sb("mT", [P, DT, N], scope=phase)
            base = [sb(f"base{i}", [P, NT, D], scope=phase) for i in range(2)]
            hWa = [sb(f"hWa{i}", [P, NT, D], scope=phase) for i in range(2)]
            split = sb("split", [P, NT, PARTS, 2, D], fp32r, scope=phase)
            zero = sb("zero", [NU - N, PARTS * BD], scope=phase)
            wide = pb("wide", [P, 4 * BANK], scope=phase)
            pairs = [pb(f"pair{i}", [P, BANK], scope=phase) for i in range(4)]

            with nc.Block() as block:
                @block.sync
                def _(sp):
                    n = 0
                    for dst, src in ((W1_sb[:, :, 0, :], W1[0:D, :].rearrange("(c p) k -> p c k", p=P)),
                                     (W1_sb[:, :, 1, :], W1[D:2 * D, :].rearrange("(c p) k -> p c k", p=P)),
                                     (Wa_sb[:], Wa.rearrange("(c p) k -> p c k", p=P)),
                                     (Wm_sb[:], Wm.rearrange("(c p) k -> p c k", p=P)),
                                     (w2_col[:, 0:1], W2[0:P, :]), (w2_col[:, 1:2], W2[P:2 * P, :]),
                                     (b1_col[:, 0:1], b1[0:P].rearrange("(k a) -> k a", a=1)),
                                     (b1_col[:, 1:2], b1[P:2 * P].rearrange("(k a) -> k a", a=1)),
                                     (w2_all[:], W2.rearrange("k a -> a k").broadcast_to([P, D])),
                                     (bias_row[:, 0, :], ba.rearrange("(a k) -> a k", a=1).broadcast_to([P, D])),
                                     (bias_row[:, 1, :], bm.rearrange("(a k) -> a k", a=1).broadcast_to([P, D])),
                                     (betas[:, 0:1], beta1.rearrange("(a k) -> a k", a=1).broadcast_to([P, 1])),
                                     (betas[:, 1:2], beta2.rearrange("(a k) -> a k", a=1).broadcast_to([P, 1])),
                                     (betas[:, 2:3], beta3.rearrange("(a k) -> a k", a=1).broadcast_to([P, 1])),
                                     (betas[:, 3:4], b2.rearrange("(a k) -> a k", a=1).broadcast_to([P, 1])),
                                     (adj_sb[:], adj.rearrange("(t p) v -> p t v", p=P))):
                        sp.dma_start(dst, src).then_inc(loaded, 16)
                        n += 16
                    sp.wait_ge(zeroed, 2)
                    sp.dma_start(u_rows[N:NU, :, :, :].rearrange("n q b k -> n (q b k)"),
                                 zero[:]).then_inc(loaded, 16)
                    sp.wait_ge(loaded, n + 16)

                @block.vector
                def _(dve):
                    nc.vector.memset(ones[:], 1.0).then_inc(zeroed, 1)
                    nc.vector.memset(zero[:], 0.0).then_inc(zeroed, 1)
                    dve.wait_ge(loaded, 17 * 16)
                    nc.vector.tensor_scalar(Wa_sb[:], Wa_sb[:], betas[:, 1:2], None, ALU.mult).then_inc(setup, 1)
                    nc.vector.tensor_scalar(Wm_sb[:], Wm_sb[:], betas[:, 2:3], None, ALU.mult).then_inc(setup, 1)
                    nc.vector.tensor_scalar(bias_row[:, 0, :], bias_row[:, 0, :], betas[:, 1:2], None,
                                            ALU.mult).then_inc(setup, 1)
                    dve.wait_ge(setup, 3)
                    nc.vector.scalar_tensor_tensor(out=bias_row[:, 0, :], in0=bias_row[:, 1, :], scalar=betas[:, 2:3],
                                                   in1=bias_row[:, 0, :], op0=ALU.mult, op1=ALU.add).then_inc(setup, 1)
                    dve.wait_ge(setup, 4)

                @block.gpsimd
                def _(pool):
                    nc.gpsimd.memset(ident[:], 0.0).then_inc(ident_step, 1)
                    pool.wait_ge(ident_step, 1)
                    nc.gpsimd.affine_select(out=ident[:], in_=ident[:], compare_op=ALU.not_equal, fill=1.0, base=0,
                                            pattern=[[-1, P]], channel_multiplier=1).then_inc(ident_step, 1)
                    pool.wait_ge(ident_step, 2)

            with ExitStack() as part:
                def row(name):
                    return sb(name, [P, D], scope=part)

                positive, major, rank_major, late, early, rank_early = map(
                    row, ("positive", "major", "rank_major", "late", "early", "rank_early"))
                place_late, place_early, place, size, scale, ones_row = map(
                    row, ("place_late", "place_early", "place", "size", "scale", "ones_row"))
                stat = sb("stat", [P, 4], scope=part)
                index = sb("index", [P, DT], scope=part)
                order_T = sb("order_T", [P, DT, D], scope=part)
                order = sb("order", [P, DT, D], scope=part)
                W1_T = sb("W1_T", [P, DT, 2 * D], scope=part)
                w2_wide = sb("w2_wide", [P, DT, P], scope=part)
                row_step = sem("row_step")
                indexed = sem("indexed")
                turned = sem("turned")
                turned_ready = sem("turned_ready")
                ordered = sem("ordered")
                ordered_ready = sem("ordered_ready")
                with nc.Block() as block:
                    @block.gpsimd
                    def _(pool):
                        nc.gpsimd.iota(index[:], pattern=[[P, DT]], base=0, channel_multiplier=1,
                                       allow_small_or_imprecise_dtypes=True).then_inc(indexed, 1)

                    @block.vector
                    def _(dve):
                        done = [0]

                        def link(ins):
                            done[0] += 1
                            ins.then_inc(row_step, 1)
                            dve.wait_ge(row_step, done[0])

                        TS, TT = nc.vector.tensor_scalar, nc.vector.tensor_tensor
                        link(nc.vector.memset(ones_row[:], 1.0))
                        link(TS(positive[:], w2_all[:], 0.0, None, ALU.is_ge))
                        link(nc.vector.tensor_reduce(stat[:, 0:1], positive[:], AX, ALU.add))
                        link(TS(stat[:, 1:2], stat[:, 0:1], float(HD), None, ALU.is_ge))
                        link(TS(sign[:], stat[:, 1:2], 2.0, -1.0, ALU.mult, ALU.add))
                        link(TS(major[:], positive[:], stat[:, 1:2], None, ALU.is_equal))
                        link(nc.vector.tensor_tensor_scan(rank_major[:], ones_row[:], major[:], 0.0, ALU.mult, ALU.add))
                        link(nc.vector.scalar_tensor_tensor(out=late[:], in0=rank_major[:], scalar=float(HD),
                                                            in1=major[:], op0=ALU.is_le, op1=ALU.mult))
                        link(TS(early[:], late[:], -1.0, 1.0, ALU.mult, ALU.add))
                        link(nc.vector.tensor_tensor_scan(rank_early[:], ones_row[:], early[:], 0.0, ALU.mult, ALU.add))
                        link(nc.vector.scalar_tensor_tensor(out=place_late[:], in0=rank_major[:], scalar=float(HD - 1),
                                                            in1=late[:], op0=ALU.add, op1=ALU.mult))
                        link(nc.vector.scalar_tensor_tensor(out=place_early[:], in0=rank_early[:], scalar=-1.0,
                                                            in1=early[:], op0=ALU.add, op1=ALU.mult))
                        link(TT(place[:], place_late[:], place_early[:], ALU.add))
                        link(TS(size[:], w2_all[:], -1.0, None, ALU.mult))
                        link(TT(size[:], size[:], w2_all[:], ALU.max))
                        link(TT(size[:], size[:], late[:], ALU.mult))
                        link(TT(scale[:], size[:], early[:], ALU.add))
                        dve.wait_ge(indexed, 1)
                        for j in range(DT):
                            link(nc.vector.scalar_tensor_tensor(out=order_T[:, j, :], in0=place[:], scalar=index[:, j:j + 1],
                                                                in1=scale[:], op0=ALU.is_equal, op1=ALU.mult))
                        for k in range(DT):
                            link(TS(w2_wide[:, k, :], ones_row[:, 0:P], w2_col[:, k:k + 1], sign[:], ALU.mult, ALU.mult))
                        dve.wait_ge(turned, 1)
                        nc.vector.tensor_copy(order[:].rearrange("p k j -> p (k j)"), pairs[0][:]).then_inc(turned_ready, 1)
                        nc.vector.tensor_copy(W1_T[:].rearrange("p k d -> p (k d)"), wide[:, 0:DT * 2 * D]).then_inc(turned_ready, 1)
                        dve.wait_ge(ordered, 1)
                        nc.vector.tensor_copy(W1_sb[:].rearrange("p c w k -> p w c k"),
                                              wide[:, 2 * BANK:4 * BANK].rearrange("p (w c k) -> p w c k", w=2, c=DT)).then_inc(ordered_ready, 1)
                        nc.vector.tensor_copy(b1_row[:], pairs[1][0:1, 0:D]).then_inc(ordered_ready, 1)
                        nc.vector.tensor_copy(w2_row[:], pairs[2][:, 0:HD]).then_inc(ordered_ready, 1)
                        dve.wait_ge(ordered_ready, 3)

                    @block.tensor
                    def _(pe):
                        for k in range(DT):
                            for w in range(2):
                                for c in range(DT):
                                    nc.tensor.transpose(wide[:, (k * 2 * DT + w * DT + c) * P:(k * 2 * DT + w * DT + c + 1) * P],
                                                        W1_sb[:, c, w, k * P:(k + 1) * P], ident[:])
                        pe.wait_ge(row_step, 17 + 2 * DT)
                        for k in range(DT):
                            for j in range(DT):
                                last = nc.tensor.transpose(pairs[0][:, k * D + j * P:k * D + (j + 1) * P],
                                                           order_T[:, j, k * P:(k + 1) * P], ident[:])
                        last.then_inc(turned, 1)
                        pe.wait_ge(turned_ready, 2)
                        for w in range(2):
                            for c in range(DT):
                                at = 2 * BANK + (w * DT + c) * D
                                for k in range(DT):
                                    nc.tensor.matmul(wide[:, at:at + D], W1_T[:, k, (w * DT + c) * P:(w * DT + c + 1) * P],
                                                     order[:, k, :], start=(k == 0), stop=(k == DT - 1))
                        for k in range(DT):
                            nc.tensor.matmul(pairs[1][0:1, 0:D], b1_col[:, k:k + 1], order[:, k, :],
                                             start=(k == 0), stop=(k == DT - 1))
                        for k in range(DT):
                            last = nc.tensor.matmul(pairs[2][:, 0:HD], w2_wide[:, k, :], order[:, k, 0:HD],
                                                    start=(k == 0), stop=(k == DT - 1))
                        last.then_inc(ordered, 1)

            h_loaded = [sem(f"h_loaded{i}") for i in range(2)]
            hT_psum = sem("hT_psum")
            hT_ready = sem("hT_ready")
            pre_psum = sem("pre_psum")
            high_ready = sem("high_ready")
            split_ready = sem("split_ready")
            hWa_psum = sem("hWa_psum")
            hWa_ready = sem("hWa_ready")
            msg_psum = sem("msg_psum")
            msg_ready = sem("msg_ready")
            scaled = sem("scaled")
            base_psum = sem("base_psum")
            base_ready = sem("base_ready")
            split_stored = sem("split_stored")
            hWa_stored = [sem(f"hWa_stored{i}") for i in range(2)]
            base_stored = [sem(f"base_stored{i}") for i in range(2)]
            node_sems = [*h_loaded, hT_psum, hT_ready, pre_psum, high_ready, split_ready, hWa_psum, hWa_ready,
                         msg_psum, msg_ready, scaled, base_psum, base_ready, split_stored, *hWa_stored, *base_stored]
            HT = NT // 2

            with nc.Block() as block:
                @block.sync
                def _(sp):
                    def load_h(b, par):
                        sp.dma_start(h[par][:], x[b, :, :].rearrange("(t p) d -> p t d", p=P)).then_inc(h_loaded[par], 16)

                    def one(b, j, par, last_round=False):
                        sp.wait_ge(split_ready, NT * (b + 1))
                        for w, rows_of in ((0, u_rows), (1, v_rows)):
                            for q in range(PARTS):
                                sp.dma_start(rows_of[0:N, q, b, :].rearrange("(t p) k -> p t k", p=P),
                                             split[:, :, q, w, :].bitcast(fp32)).then_inc(split_stored, 16)
                        sp.wait_ge(hWa_ready, HT * (b + 1))
                        sp.dma_start(hWa_dram[b, :, :].rearrange("(t p) d -> p t d", p=P), hWa[par][:]).then_inc(hWa_stored[par], 16)
                        sp.wait_ge(base_ready, HT * (b + 1))
                        sp.dma_start(base_dram[b, :, :].rearrange("(t p) d -> p t d", p=P), base[par][:]).then_inc(base_stored[par], 16)
                        if not last_round:
                            load_h(b + 2, par)

                    for par in range(2):
                        load_h(par, par)
                    for par in range(2):
                        one(par, 0, par)
                    with sp.Fori(1, B // 2 - 1) as j:
                        for par in range(2):
                            one(j * 2 + par, j, par)
                    for par in range(2):
                        one(B - 2 + par, B // 2 - 1, par, True)
                    sp.wait_ge(split_stored, 16 * 2 * PARTS * B)
                    for par in range(2):
                        sp.wait_ge(hWa_stored[par], 16 * (B // 2))
                        sp.wait_ge(base_stored[par], 16 * (B // 2))

                @block.tensor
                def _(pe):
                    def one(b, j, par):
                        pe.wait_ge(h_loaded[par], 16 * (j + 1))
                        waits(pe, msg_ready, b * DT)
                        for c in range(DT):
                            for t in range(NT):
                                last = nc.tensor.transpose(wide[:, c * N + t * P:c * N + (t + 1) * P],
                                                           h[par][:, t, c * P:(c + 1) * P], ident[:])
                            last.then_inc(hT_psum, 1)
                        pe.wait_ge(hT_ready, DT * (b + 1))
                        waits(pe, base_ready, b * HT)
                        for t in range(NT):
                            if t >= 4:
                                pe.wait_ge(split_ready, b * NT + (t - 3))
                            bank = pairs[t % 4]
                            for c in range(DT):
                                nc.tensor.matmul(bank[:], hT[:, c, t * P:(t + 1) * P],
                                                 W1_sb[:, c, :, :].rearrange("p w k -> p (w k)"),
                                                 start=(c == 0), stop=False)
                            nc.tensor.matmul(bank[:, D:2 * D], ones[0:1, :], b1_row[0:1, :],
                                             start=False, stop=True).then_inc(pre_psum, 1)
                        for c in range(DT):
                            for n in range(N // BANK):
                                for t in range(NT):
                                    last = nc.tensor.matmul(wide[:, c * N + n * BANK:c * N + (n + 1) * BANK],
                                                            h[par][:, t, c * P:(c + 1) * P],
                                                            adj_sb[:, t, n * BANK:(n + 1) * BANK],
                                                            start=(t == 0), stop=(t == NT - 1))
                            last.then_inc(msg_psum, 1)
                        for t in range(NT):
                            if t % 2 == 0:
                                pe.wait_ge(split_ready, b * NT + (HT + t // 2 + 1))
                            for c in range(DT):
                                last = nc.tensor.matmul(pairs[t // 2][:, (t % 2) * D:(t % 2 + 1) * D],
                                                        hT[:, c, t * P:(t + 1) * P], Wa_sb[:, c, :],
                                                        start=(c == 0), stop=(c == DT - 1))
                            if t % 2:
                                last.then_inc(hWa_psum, 1)
                        pe.wait_ge(msg_ready, DT * (b + 1))
                        for t in range(NT):
                            if t % 2 == 0:
                                pe.wait_ge(hWa_ready, b * HT + (t // 2 + 1))
                            for c in range(DT):
                                last = nc.tensor.matmul(pairs[t // 2][:, (t % 2) * D:(t % 2 + 1) * D],
                                                        mT[:, c, t * P:(t + 1) * P], Wm_sb[:, c, :],
                                                        start=(c == 0), stop=(c == DT - 1))
                            if t % 2:
                                last.then_inc(base_psum, 1)

                    each_batch(pe, one)

                @block.scalar
                def _(act):
                    def one(b, j, par):
                        act.wait_ge(hT_psum, b * DT + 1)
                        nc.scalar.copy(hT[:, 0, :], wide[:, 0:N]).then_inc(hT_ready, 1)
                        waits(act, split_stored, b * (16 * 2 * PARTS))
                        for t in range(NT):
                            act.wait_ge(pre_psum, b * NT + (t + 1))
                            nc.scalar.copy(split[:, t, 0, :, :].rearrange("p w k -> p (w k)"),
                                           pairs[t % 4][:]).then_inc(high_ready, 1)
                        waits(act, hWa_stored[par], j * 16)
                        for t in range(HT):
                            act.wait_ge(hWa_psum, b * HT + (t + 1))
                            nc.scalar.copy(hWa[par][:, 2 * t:2 * t + 2, :].rearrange("p t k -> p (t k)"),
                                           pairs[t][:]).then_inc(hWa_ready, 1)

                    each_batch(act, one)

                @block.vector
                def _(dve):
                    def one(b, j, par):
                        dve.wait_ge(hT_psum, b * DT + 2)
                        nc.vector.tensor_copy(hT[:, 1, :], wide[:, N:2 * N]).then_inc(hT_ready, 1)
                        for t in range(NT):
                            dve.wait_ge(high_ready, b * NT + (t + 1))
                            nc.vector.tensor_tensor(split[:, t, 1, :, :].rearrange("p w k -> p (w k)"), pairs[t % 4][:],
                                                    split[:, t, 0, :, :].rearrange("p w k -> p (w k)").bitcast(fp32),
                                                    ALU.subtract).then_inc(split_ready, 1)
                        for c in range(DT):
                            dve.wait_ge(msg_psum, b * DT + (c + 1))
                            nc.vector.tensor_tensor(mT[:, c, :], wide[:, c * N:(c + 1) * N], hT[:, c, :],
                                                    ALU.mult).then_inc(msg_ready, 1)
                        dve.wait_ge(scaled, 2 * (b + 1))
                        for t in range(HT):
                            dve.wait_ge(base_psum, b * HT + (t + 1))
                            rows_ = base[par][:, 2 * t:2 * t + 2, :].rearrange("p t k -> p (t k)")
                            nc.vector.tensor_tensor(rows_, rows_, pairs[t][:], ALU.add).then_inc(base_ready, 1)

                    each_batch(dve, one)

                @block.gpsimd
                def _(pool):
                    def one(b, j, par):
                        pool.wait_ge(h_loaded[par], 16 * (j + 1))
                        waits(pool, base_stored[par], j * 16)
                        nc.gpsimd.tensor_tensor(base[par][:], h[par][:], betas[:, 0:1].rearrange("p (a k) -> p a k", a=1)
                                                .broadcast_to([P, NT, D]), ALU.mult).then_inc(scaled, 1)
                        pool.wait_ge(scaled, b * 2 + 1)
                        nc.gpsimd.tensor_tensor(base[par][:], base[par][:],
                                                bias_row[:, 0, :].rearrange("p (a k) -> p a k", a=1).broadcast_to([P, NT, D]),
                                                ALU.add).then_inc(scaled, 1)

                    each_batch(pool, one)
            finish_step(node_sems)

        edges = ctx.enter_context(ExitStack())
        adj_u = sb("adj_u", [UB, ST, N], scope=edges)
        rank_end = sb("rank_end", [UB, ST * N + AHEAD * VB], scope=edges)
        row_start = sb("row_start", [UB, ST * NB + AHEAD], scope=edges)
        row_end = sb("row_end", [UB, ST * NB + AHEAD], scope=edges)
        slot_row = sb("slot_row", [UB, SLOTS], scope=edges)
        slot_col = sb("slot_col", [P, TILES, VB], scope=edges)
        passes_i = sb("passes_i", [1, 1], i32, scope=edges)

        with ExitStack() as phase:
            is_edge = sb("is_edge", [UB, ST * N], scope=phase)
            restart = sb("restart", [UB, N], scope=phase)
            above = sb("above", [UB, UB], scope=phase)
            counts = sb("counts", [UB, ST * NB], scope=phase)
            ones_col = sb("ones_col", [UB, 1], scope=phase)
            full = sb("full", [1, 4], scope=phase)
            levels = sb("levels", [1, PASSES], scope=phase)
            over = sb("over", [1, PASSES], scope=phase)
            start_psum = pb("start_psum", [UB, BANK], scope=phase)
            total_psum = pb("total_psum", [1, BANK], scope=phase)
            a_loaded = sem("a_loaded")
            a_zero = sem("a_zero")
            consts = sem("consts")
            step = sem("step")
            counted = sem("counted")
            summed = sem("summed")
            with nc.Block() as block:
                @block.sync
                def _(sp):
                    whole = N // UB
                    sp.dma_start(adj_u[:, 0:whole, :],
                                 adj[0:whole * UB, :].rearrange("(s p) v -> p s v", p=UB)).then_inc(a_loaded, 16)
                    sp.wait_ge(a_zero, 1)
                    sp.dma_start(adj_u[0:N - whole * UB, whole, :], adj[whole * UB:N, :]).then_inc(a_loaded, 16)
                    sp.wait_ge(a_loaded, 32)

                @block.gpsimd
                def _(pool):
                    nc.gpsimd.memset(above[:], 0.0).then_inc(consts, 1)
                    pool.wait_ge(consts, 1)
                    nc.gpsimd.affine_select(out=above[:], in_=above[:], compare_op=ALU.is_ge, fill=1.0, base=0,
                                            pattern=[[-1, UB]], channel_multiplier=1).then_inc(consts, 1)
                    nc.gpsimd.iota(slot_row[:], pattern=[[1, SLOTS]], base=0, channel_multiplier=0,
                                   allow_small_or_imprecise_dtypes=True).then_inc(consts, 1)
                    nc.gpsimd.iota(slot_col[:], pattern=[[P, TILES], [0, VB]], base=1, channel_multiplier=1,
                                   allow_small_or_imprecise_dtypes=True).then_inc(consts, 1)
                    nc.gpsimd.iota(levels[:], pattern=[[SLOTS, PASSES]], base=0, channel_multiplier=0,
                                   allow_small_or_imprecise_dtypes=True).then_inc(consts, 1)

                @block.vector
                def _(dve):
                    done = [0]

                    def link(ins):
                        done[0] += 1
                        ins.then_inc(step, 1)
                        dve.wait_ge(step, done[0])

                    nc.vector.memset(adj_u[:, ST - 1, :], 0.0).then_inc(a_zero, 1)
                    link(nc.vector.memset(restart[:], 1.0))
                    link(nc.vector.memset(restart[:].rearrange("p (n w) -> p n w", w=VB)[:, :, 0:1], 0.0))
                    link(nc.vector.memset(ones_col[:], 1.0))
                    link(nc.vector.memset(rank_end[:, ST * N:], 0.0))
                    link(nc.vector.memset(row_start[:, ST * NB:], 0.0))
                    link(nc.vector.memset(row_end[:, ST * NB:], 0.0))
                    dve.wait_ge(a_loaded, 32)
                    link(nc.vector.tensor_scalar(is_edge[:], adj_u[:].rearrange("p s v -> p (s v)"), 0.0, None, ALU.not_equal))
                    for s in range(ST):
                        link(nc.vector.tensor_tensor_scan(rank_end[:, s * N:(s + 1) * N], restart[:],
                                                          is_edge[:, s * N:(s + 1) * N], 0.0, ALU.mult, ALU.add))
                    link(nc.vector.tensor_copy(counts[:], rank_end[:, 0:ST * N].rearrange("p (n w) -> p n w", w=VB)[:, :, VB - 1]))
                    nc.vector.memset(full[:], 0.0).then_inc(counted, 1)
                    link(nc.vector.tensor_tensor(rank_end[:, 0:ST * N], rank_end[:, 0:ST * N], is_edge[:], ALU.mult))
                    dve.wait_ge(summed, 1)
                    link(nc.vector.tensor_copy(row_start[:, 0:ST * NB], start_psum[:, 0:ST * NB]))
                    link(nc.vector.tensor_tensor(row_end[:, 0:ST * NB], row_start[:, 0:ST * NB], counts[:], ALU.add))
                    blocks = rank_end[:, 0:ST * N].rearrange("p (n w) -> p n w", w=VB)
                    link(nc.vector.tensor_tensor(blocks, blocks,
                                                 row_start[:, 0:ST * NB].rearrange("p (n a) -> p n a", a=1).broadcast_to([UB, ST * NB, VB]),
                                                 ALU.add))
                    link(nc.vector.tensor_reduce(full[:, 0:1], total_psum[0:1, 0:ST * NB], AX, ALU.max))
                    dve.wait_ge(consts, 5)
                    link(nc.vector.tensor_scalar(over[:], levels[:], full[:, 0:1], None, ALU.is_lt))
                    link(nc.vector.tensor_reduce(full[:, 1:2], over[:], AX, ALU.add))
                    link(nc.vector.tensor_copy(passes_i[:], full[:, 1:2]))

                @block.tensor
                def _(pe):
                    pe.wait_ge(counted, 1)
                    pe.wait_ge(consts, 2)
                    nc.tensor.matmul(start_psum[:, 0:ST * NB], above[:], counts[:], start=True, stop=True)
                    nc.tensor.matmul(total_psum[0:1, 0:ST * NB], ones_col[:], counts[:], start=True, stop=True).then_inc(summed, 1)

        passes = nc.values_load(passes_i[0:1, 0:1], min_val=0, max_val=PASSES)

        rows = [sb(f"rows{i}", [P, PARTS, BD], fp32r, scope=edges) for i in range(2)]
        pick = [sb(f"pick{i}", [P, SLOTS], fp32r, scope=edges) for i in range(TURNS)]
        ge_start = sb("ge_start", [UB, SLOTS], scope=edges)
        u_of_slot = [sb(f"u_of_slot{i}", [P, TILES, UB], scope=edges) for i in range(TURNS)]
        v_of_slot = [sb(f"v_of_slot{i}", [P, TILES, VB], scope=edges) for i in range(TURNS)]
        junk = {e: sb(f"junk_{e}", [P, RING[e], BPC, HD], scope=edges) for e in ("dve", "act")}
        score = [sb(f"score{i}", [P, 2, TILES, B], scope=edges) for i in range(2)]
        total = [sb(f"total{i}", [P, TILES, B], scope=edges) for i in range(2)]
        gate = [sb(f"gate{i}", [P, TILES, B], scope=edges) for i in range(2)]
        spread = [sb(f"spread{i}", [P, TILES, B, VB], scope=edges) for i in range(2)]
        placed = [sb(f"placed{i}", [UB, B, VB], scope=edges) for i in range(2)]
        gated = sb("gated", [UB, B, 2 * VB], scope=edges)
        earlier = sb("earlier", [UB, B, 2 * VB], scope=edges)
        with ExitStack() as phase:
            gather = {e: [pb(f"gather_{e}{i}", [P, BANK], scope=phase) for i in range(RING[e])] for e in RING}
            FLIP_U, FLIP_V = TILES * VB, TILES * (VB + UB)
            pick_psum = pb("pick_psum", [P, FLIP_V + SLOTS], scope=phase)
            place_psum = [pb(f"place_psum{i}", [UB, BANK], scope=phase) for i in range(2)]

            rows_loaded = [[sem(f"rows_loaded{par}_{c}") for c in range(CH)] for par in range(2)]
            pick_u_part = sem("pick_u_part")
            pick_u = sem("pick_u")
            ranked = sem("ranked")
            v_picked = sem("v_picked")
            flipped = sem("flipped")
            picks_ready = sem("picks_ready")
            gathered = {e: sem(f"gathered_{e}") for e in ("dve", "act")}
            scored = {e: sem(f"scored_{e}") for e in ("dve", "act")}
            totalled = sem("totalled")
            gated_slots = sem("gated_slots")
            spread_ready = sem("spread_ready")
            placed_psum = sem("placed_psum")
            placed_ready = sem("placed_ready")
            masked = sem("masked")
            gate_stored = sem("gate_stored")
            earlier_loaded = sem("earlier_loaded")
            merged = sem("merged")
            edge_sems = [*rows_loaded[0], *rows_loaded[1], pick_u_part, pick_u, ranked, v_picked, flipped, picks_ready,
                         *gathered.values(), *scored.values(), totalled,
                         gated_slots, spread_ready, placed_psum, placed_ready, masked, gate_stored,
                         earlier_loaded, merged]

            def strip(s, first):
                with nc.Block() as block:
                    def first_block(n):
                        return isinstance(n, int) and n == 0

                    def each_block(eng, one):
                        for i in range(TURNS):
                            one(i, i // 2, i)
                        with eng.Fori(1, NB // TURNS) as g:
                            for i in range(TURNS):
                                one(g * TURNS + i, g * (TURNS // 2) + i // 2, i)

                    def load(sp, part, source, par, c):
                        sp.dma_start(rows[par][part, :, c * BPC * D:(c + 1) * BPC * D].bitcast(fp32),
                                     source[:, :, c * BPC:(c + 1) * BPC, :].rearrange("n q b k -> n q (b k)")).then_inc(rows_loaded[par][c], 16)

                    def load_v(sp, n, par, c):
                        load(sp, slice(UB, P), v_rows[bass.ds(n * VB, VB), :, :, :], par, c)

                    def store(sp, j):
                        place_ = gate_dram[:, bass.ds(s * UB, UB), bass.ds(j * 2 * VB, 2 * VB)].rearrange("b u v -> u b v")
                        waits(sp, masked, (j + 1) * 2)
                        if not first:
                            sp.dma_start(earlier[:], place_).then_inc(earlier_loaded, 16)
                            waits(sp, merged, j + 1)
                        sp.dma_start(place_, gated[:]).then_inc(gate_stored, 16)

                    @block.sync
                    def _(sp):
                        for par in range(2):
                            for c in range(CH):
                                load(sp, slice(0, UB), u_rows[bass.ds(s * UB, UB), :, :, :], par, c)
                                load_v(sp, par, par, c)
                        for par in range(2):
                            sp.wait_ge(gathered[LAST], N_OF[LAST] * (par + 1))
                            for c in range(CH):
                                load_v(sp, par + 2, par, c)
                        with sp.Fori(1, NB // 2 - 1) as j:
                            for par in range(2):
                                sp.wait_ge(gathered[LAST], j * (2 * N_OF[LAST]) + N_OF[LAST] * (par + 1))
                                for c in range(CH):
                                    load_v(sp, j * 2 + (2 + par), par, c)
                                if par == 0:
                                    store(sp, j - 1)
                        for j in (NB // 2 - 2, NB // 2 - 1):
                            store(sp, j)
                        sp.wait_ge(gate_stored, 16 * (NB // 2))

                    @block.tensor
                    def _(pe):
                        def rank(n, i):
                            waits(pe, pick_u, n + 1)
                            waits(pe, picks_ready, 2 * n)
                            for t in range(TILES):
                                last = nc.tensor.matmul(pick_psum[:, t * VB:(t + 1) * VB],
                                                        pick[i][0:UB, t * P:(t + 1) * P].bitcast(fp32),
                                                        rank_end[:, bass.ds(s * N + n * VB, VB)], start=True, stop=True)
                            last.then_inc(ranked, 1)

                        def flip(n, i):
                            waits(pe, v_picked, n + 1)
                            for t in range(TILES):
                                nc.tensor.transpose(pick_psum[:, FLIP_U + t * UB:FLIP_U + (t + 1) * UB],
                                                    pick[i][0:UB, t * P:(t + 1) * P].bitcast(fp32), ident[0:UB, 0:UB])
                            for t in range(TILES):
                                last = nc.tensor.matmul(pick_psum[UB:P, FLIP_V + t * P:FLIP_V + (t + 1) * P],
                                                        v_of_slot[i][:, t, :], ident[:], start=True, stop=True)
                            last.then_inc(flipped, 1)

                        def place(n, i):
                            par = i % 2
                            waits(pe, spread_ready, TILES * (n + 1))
                            waits(pe, placed_ready, n - 1 if isinstance(n, int) else n + (-1))
                            for t in range(TILES):
                                last = nc.tensor.matmul(place_psum[par][:], u_of_slot[i][:, t, :],
                                                        spread[par][:, t, :, :].rearrange("p b v -> p (b v)"),
                                                        start=(t == 0), stop=(t == TILES - 1))
                            last.then_inc(placed_psum, 1)

                        def one(n, j, i):
                            par = i % 2
                            waits(pe, picks_ready, 2 * (n + 1))
                            count = {"dve": 0, "act": 0}
                            for unit, (c, half, t) in enumerate(UNITS):
                                e = OWNER[unit]
                                if unit == 7:
                                    rank(n + AHEAD, (i + AHEAD) % TURNS)
                                if unit == 14:
                                    flip(n + AHEAD, (i + AHEAD) % TURNS)
                                if unit == 12 and not first_block(n):
                                    place(n + (-1), (i - 1) % TURNS)
                                if half == 0 and t == 0:
                                    waits(pe, rows_loaded[par][c], 16 * (j + 2))
                                if not isinstance(n, int) or n * N_OF[e] + count[e] >= RING[e]:
                                    waits(pe, scored[e], n * N_OF[e] + (count[e] - RING[e] + 1))
                                bank = gather[e][(par * N_OF[e] + count[e]) % RING[e]]
                                for q in range(PARTS):
                                    last = nc.tensor.matmul(
                                        bank[:], pick[i][:, t * P:(t + 1) * P],
                                        rows[par][:, q, c * BPC * D:(c + 1) * BPC * D]
                                        .rearrange("p (b h k) -> p b h k", b=BPC, h=2)[:, :, half, :],
                                        start=(q == 0), stop=(q == PARTS - 1))
                                last.then_inc(gathered[e], 1)
                                count[e] += 1

                        for n in range(AHEAD):
                            rank(n, n)
                            flip(n, n)
                        each_block(pe, one)
                        place(NB - 1, TURNS - 1)

                    @block.vector
                    def _(dve):
                        def pick_rows(n, i):
                            col = s * NB + n
                            waits(dve, gathered[LAST], n * N_OF[LAST] + (1 - TURNS) * N_OF[LAST])
                            nc.vector.tensor_scalar(ge_start[:], slot_row[:], row_start[:, bass.ds(col, 1)], None,
                                                    ALU.is_ge).then_inc(pick_u_part, 1)
                            waits(dve, pick_u_part, n + 1)
                            nc.vector.scalar_tensor_tensor(out=pick[i][0:UB, :], in0=slot_row[:],
                                                           scalar=row_end[:, bass.ds(col, 1)], in1=ge_start[:],
                                                           op0=ALU.is_lt, op1=ALU.mult).then_inc(pick_u, 1)

                        def pick_columns(n, i):
                            waits(dve, ranked, n + 1)
                            waits(dve, spread_ready, n * TILES + (1 - TURNS) * TILES)
                            nc.vector.tensor_tensor(v_of_slot[i][:], pick_psum[:, 0:TILES * VB].rearrange("p (t v) -> p t v", t=TILES),
                                                    slot_col[:], ALU.is_equal).then_inc(v_picked, 1)

                        def one(n, j, i):
                            par = i % 2
                            pick_rows(n + AHEAD, (i + AHEAD) % TURNS)
                            waits(dve, totalled, n + (-1))
                            mine = 0
                            for unit, (c, half, t) in enumerate(UNITS):
                                if unit == 11:
                                    pick_columns(n + AHEAD, (i + AHEAD) % TURNS)
                                if OWNER[unit] != "dve":
                                    continue
                                waits(dve, gathered["dve"], n * N_OF["dve"] + (mine + 1))
                                waits(dve, scored["dve"], n * N_OF["dve"] + (mine - RING["dve"] + 1))
                                turn = (par * N_OF["dve"] + mine) % RING["dve"]
                                bank = gather["dve"][turn]
                                for k in range(BPC):
                                    b_ = c * BPC + k
                                    sums = score[par][:, half, t, b_:b_ + 1]
                                    if half == 0:
                                        ins = nc.vector.scalar_tensor_tensor(
                                            out=junk["dve"][:, turn, k, :], in0=bank[:, k * HD:(k + 1) * HD],
                                            scalar=0.0, in1=w2_row[:], op0=ALU.max, op1=ALU.mult, accum_out=sums)
                                    else:
                                        ins = nc.vector.tensor_scalar(
                                            junk["dve"][:, turn, k, :], bank[:, k * HD:(k + 1) * HD],
                                            0.0, None, ALU.max, ALU.add, accum_out=sums)
                                ins.then_inc(scored["dve"], 1)
                                mine += 1

                        for n in range(AHEAD):
                            pick_rows(n, n)
                            pick_columns(n, n)
                        each_block(dve, one)

                    @block.scalar
                    def _(act):
                        def sigmoid(n, par):
                            waits(act, totalled, n + 1)
                            waits(act, spread_ready, n * TILES + (-TILES))
                            nc.scalar.activation(gate[par][:], total[par][:], ACT.Sigmoid, bias=betas[:, 3:4],
                                                 scale=sign[:]).then_inc(gated_slots, 1)

                        def take_placed(n, par):
                            waits(act, placed_psum, n + 1)
                            waits(act, masked, n + (-1))
                            nc.scalar.copy(placed[par][:].rearrange("p b v -> p (b v)"), place_psum[par][:]).then_inc(placed_ready, 1)

                        def take_picks(n, i):
                            waits(act, flipped, n + 1)
                            waits(act, placed_psum, n + (1 - TURNS))
                            nc.scalar.copy(u_of_slot[i][:].rearrange("p t u -> p (t u)"), pick_psum[:, FLIP_U:FLIP_V]).then_inc(picks_ready, 1)
                            nc.scalar.copy(pick[i][UB:P, :], pick_psum[UB:P, FLIP_V:FLIP_V + SLOTS]).then_inc(picks_ready, 1)

                        def one(n, j, i):
                            par = i % 2
                            prev, prev_n = not first_block(n), n + (-1)
                            waits(act, totalled, n + (-1))
                            mine = 0
                            for unit, (c, half, t) in enumerate(UNITS):
                                if unit == 3 and prev:
                                    sigmoid(prev_n, 1 - par)
                                if unit == 1:
                                    take_picks(n + 1, (i + 1) % TURNS)
                                if OWNER[unit] != "act":
                                    continue
                                waits(act, gathered["act"], n * N_OF["act"] + (mine + 1))
                                waits(act, scored["act"], n * N_OF["act"] + (mine - RING["act"] + 1))
                                turn = (par * N_OF["act"] + mine) % RING["act"]
                                bank = gather["act"][turn]
                                for k in range(BPC):
                                    b_ = c * BPC + k
                                    ins = nc.scalar.activation(junk["act"][:, turn, k, :],
                                                               bank[:, k * HD:(k + 1) * HD], ACT.Relu,
                                                               accum_out=score[par][:, half, t, b_:b_ + 1])
                                ins.then_inc(scored["act"], 1)
                                mine += 1
                            if prev:
                                take_placed(prev_n, 1 - par)

                        take_picks(0, 0)
                        each_block(act, one)
                        sigmoid(NB - 1, 1)
                        take_placed(NB - 1, 1)

                    @block.gpsimd
                    def _(pool):
                        def add_halves(n, par):
                            for e in scored:
                                waits(pool, scored[e], (n + 1) * N_OF[e])
                            waits(pool, gated_slots, n + (-1))
                            nc.gpsimd.tensor_tensor(total[par][:], score[par][:, 0, :, :], score[par][:, 1, :, :],
                                                    ALU.add).then_inc(totalled, 1)

                        def spread_gates(n, i):
                            par = i % 2
                            add_halves(n, par)
                            waits(pool, gated_slots, n + 1)
                            waits(pool, placed_psum, n + (-1))
                            for t in range(TILES):
                                nc.gpsimd.tensor_tensor(
                                    spread[par][:, t, :, :],
                                    v_of_slot[i][:, t, :].rearrange("p (a v) -> p a v", a=1).broadcast_to([P, B, VB]),
                                    gate[par][:, t, :].rearrange("p (b a) -> p b a", a=1).broadcast_to([P, B, VB]),
                                    ALU.mult).then_inc(spread_ready, 1)

                        def mask(n, j, i):
                            par = i % 2
                            waits(pool, placed_ready, n + 1)
                            if par == 0:
                                waits(pool, gate_stored, 16 * j)
                            nc.gpsimd.tensor_tensor(
                                gated[:, :, par * VB:(par + 1) * VB], placed[par][:],
                                adj_u[:].rearrange("p s v -> p (s v)")[:, bass.ds(s * N + n * VB, VB)]
                                .rearrange("p (a v) -> p a v", a=1).broadcast_to([UB, B, VB]),
                                ALU.mult).then_inc(masked, 1)
                            if par == 1 and not first:
                                waits(pool, masked, n + 1)
                                waits(pool, earlier_loaded, 16 * (j + 1))
                                nc.gpsimd.tensor_tensor(gated[:], gated[:], earlier[:], ALU.add).then_inc(merged, 1)

                        def one(n, j, i):
                            spread_gates(n, i)
                            mask(n, j, i)

                        each_block(pool, one)
                finish_step(edge_sems)

            with nc.Fori(0, ST) as s:
                strip(s, True)
            shifted = sem("shifted")
            with nc.If(passes > 1):
                with nc.Fori(1, passes):
                    with nc.Block() as block:
                        @block.vector
                        def _(dve):
                            nc.vector.tensor_scalar(slot_row[:], slot_row[:], float(SLOTS), None, ALU.add).then_inc(shifted, 1)
                            nc.vector.tensor_scalar(slot_col[:], slot_col[:], float(SLOTS), None, ALU.add).then_inc(shifted, 1)
                            dve.wait_ge(shifted, 2)
                    finish_step([shifted])
                    with nc.Fori(0, ST) as s:
                        strip(s, False)
                    finish_step([shifted])
        edges.close()

        with ExitStack() as phase:
            gate_b = [sb(f"gate_b{i}", [P, NT, N], scope=phase) for i in range(2)]
            hWa_b = [sb(f"hWa_b{i}", [P, NT, D], scope=phase) for i in range(2)]
            z = [sb(f"z{i}", [P, NT, D], scope=phase) for i in range(2)]
            z_psum = [[pb(f"z_psum{par}_{i}", [P, BANK], scope=phase) for i in range(NT // 2)] for par in range(2)]
            gate_loaded = [[sem(f"gate_loaded{par}_{i}") for i in range(NT // 2)] for par in range(2)]
            hWa_loaded = [sem(f"hWa_loaded{i}") for i in range(2)]
            z_loaded = [sem(f"z_loaded{i}") for i in range(2)]
            z_summed = sem("z_summed")
            z_ready = sem("z_ready")
            z_stored = [sem(f"z_stored{i}") for i in range(2)]
            HT = NT // 2
            with nc.Block() as block:
                @block.sync
                def _(sp):
                    def one(b, j, par):
                        waits(sp, z_summed, b * HT + (-HT))
                        sp.dma_start(hWa_b[par][:], hWa_dram[b, :, :].rearrange("(t p) d -> p t d", p=P)).then_inc(hWa_loaded[par], 16)
                        for i in range(HT):
                            sp.dma_start(gate_b[par][:, 2 * i:2 * i + 2, :],
                                         gate_dram[b, 2 * i * P:2 * (i + 1) * P, :].rearrange("(t p) v -> p t v", p=P)).then_inc(gate_loaded[par][i], 16)
                        waits(sp, z_stored[par], j * 16)
                        sp.dma_start(z[par][:], base_dram[b, :, :].rearrange("(t p) d -> p t d", p=P)).then_inc(z_loaded[par], 16)

                    each_batch(sp, one)

                @block.scalar
                def _(act):
                    def one(b, j, par):
                        act.wait_ge(z_ready, HT * (b + 1))
                        act.dma_start(out[b, :, :].rearrange("(t p) d -> p t d", p=P), z[par][:]).then_inc(z_stored[par], 16)

                    each_batch(act, one)
                    for par in range(2):
                        act.wait_ge(z_stored[par], 16 * (B // 2))

                @block.tensor
                def _(pe):
                    def one(b, j, par):
                        pe.wait_ge(hWa_loaded[par], 16 * (j + 1))
                        waits(pe, z_ready, b * HT + (-HT))
                        for v in range(NT):
                            for t in range(NT):
                                if v == 0 and t % 2 == 0:
                                    pe.wait_ge(gate_loaded[par][t // 2], 16 * (j + 1))
                                last = nc.tensor.matmul(z_psum[par][v // 2][:, (v % 2) * D:(v % 2 + 1) * D],
                                                        gate_b[par][:, t, v * P:(v + 1) * P], hWa_b[par][:, t, :],
                                                        start=(t == 0), stop=(t == NT - 1))
                            if v % 2:
                                last.then_inc(z_summed, 1)

                    each_batch(pe, one)

                @block.vector
                def _(dve):
                    def one(b, j, par):
                        dve.wait_ge(z_loaded[par], 16 * (j + 1))
                        for t in range(HT):
                            dve.wait_ge(z_summed, b * HT + (t + 1))
                            rows_ = z[par][:, 2 * t:2 * t + 2, :].rearrange("p t k -> p (t k)")
                            nc.vector.tensor_tensor(rows_, rows_, z_psum[par][t][:], ALU.add).then_inc(z_ready, 1)

                    each_batch(dve, one)


_INS = ['x', 'adj', 'L0_gnn_W1', 'L0_gnn_b1', 'L0_gnn_W2', 'L0_gnn_b2', 'L0_gnn_Wa', 'L0_gnn_ba', 'L0_gnn_Wm',
        'L0_gnn_bm', 'L0_gnn_beta1', 'L0_gnn_beta2', 'L0_gnn_beta3']
_OUTS = [((16, 1024, 256), 'float32')]


def kernel(**inputs):
    import numpy as _np
    import concourse.bacc as _bacc
    from concourse import mybir as _mybir
    from concourse.bass_utils import run_bass_kernel_spmd as _run

    nc = _bacc.Bacc("TRN2", target_bir_lowering=False, num_devices=1)
    arrays, args = {}, []
    for name in _INS:
        a = _np.asarray(inputs[name])
        a = _np.ascontiguousarray(a.reshape(1) if a.ndim == 0 else a)
        arrays[f"in_{name}_dram"] = a
        args.append(nc.dram_tensor(f"in_{name}_dram", a.shape, _mybir.dt.from_np(a.dtype), kind="ExternalInput").ap())
    for i, (shape, dtype) in enumerate(_OUTS):
        dt = _mybir.dt.from_np(_np.dtype(dtype))
        args.append(nc.dram_tensor(f"out_{i}_dram", shape, dt, kind="ExternalOutput").ap())
    gnn_edges_kernel(nc, *args)
    r = _run(nc, [arrays], core_ids=[0])
    got = tuple(r.results[0][f"out_{i}_dram"] for i in range(len(_OUTS)))
    return got[0]
```
